# Optimizing a Trainium2 kernel written in Bass

```python
import numpy as np
import jax
import jax.numpy as jnp

def _softmax(x, axis=-1):
    return jax.nn.softmax(x, axis=axis)

def _gelu(x):
    return jax.nn.gelu(x, approximate=True)

def _silu(x):
    return jax.nn.silu(x)

def _sigmoid(x):
    return jax.nn.sigmoid(x)

def _layernorm(x, axis=-1, eps=1e-05):
    m = jnp.mean(x, axis=axis, keepdims=True)
    v = jnp.var(x, axis=axis, keepdims=True)
    return (x - m) / jnp.sqrt(v + eps)

def _scatter_add(tgt, idx, src, axis=0):
    return tgt.at[idx].add(src)

def _segment_sum(src, seg, n):
    return jax.ops.segment_sum(src, seg, n)
kernel_name = 'mk_flamingo_gated_d1_seqx_r8_68d43a'

def setup_inputs(seed: int=0):
    np.random.seed(seed)
    _w = jnp.asarray

    def _rec_inputs():
        import jax
        import jax.numpy as jnp
        _rk = jax.random.key(seed)
        x = -0.0002928 + 1 * jax.random.normal(jax.random.fold_in(_rk, 1), (32, 128, 128), jnp.float32)
        _lenS = 128 - jax.random.randint(jax.random.fold_in(_rk, 7), (32,), 0, max(1, 128 // 4) + 1, jnp.int32)
        _lenS2 = 128 - jax.random.randint(jax.random.fold_in(_rk, 8), (32,), 0, max(1, 128 // 4) + 1, jnp.int32)
        _ctx_1024P = jax.random.normal(jax.random.fold_in(_rk, 11), (32, 16, 128), jnp.float32)
        _ctx_1024c = jax.random.dirichlet(jax.random.fold_in(_rk, 511), 0.3 * jnp.ones((16,), jnp.float32), (32, 128))
        _ctx_1024t = jnp.einsum('bsk,bkd->bsd', _ctx_1024c, _ctx_1024P)
        _ctx_1024t = _ctx_1024t * jax.lax.rsqrt(jnp.mean(jnp.square(_ctx_1024t)) + 1e-12) * 0.953939
        ctx_1024 = -1.39393e-06 + 0.999914 * (_ctx_1024t + 0.3 * jax.random.normal(jax.random.fold_in(_rk, 611), (32, 128, 128), jnp.float32))
        _g = jax.random.normal(jax.random.fold_in(_rk, 9001), (2, 1), jnp.float32)
        _g = jnp.sign(_g) * jnp.maximum(jnp.abs(_g), 1.0) + (_g == 0) * 1.0
        g_xattn = _g[0]
        g_ffn = _g[1]
        return (x, ctx_1024, g_xattn, g_ffn)
    x, ctx_1024, g_xattn, g_ffn = _rec_inputs()

    def _L0_xattn_setup():
        import jax, jax.numpy as jnp
        import numpy as np
        DIM = 128
        N_HEADS = 16
        HEAD_DIM = DIM // N_HEADS
        B, N, M = (2, 256, 256)
        key = jax.random.key(seed)
        ks = jax.random.split(key, 10)
        s = 1.0 / np.sqrt(DIM)
        return {'x1': jax.random.normal(ks[0], (B, N, DIM), dtype=jnp.float32), 'x2': jax.random.normal(ks[1], (B, M, DIM), dtype=jnp.float32), 'Wq': jax.random.normal(ks[2], (DIM, DIM), dtype=jnp.float32) * s, 'bq': jnp.zeros((DIM,), dtype=jnp.float32), 'Wk': jax.random.normal(ks[3], (DIM, DIM), dtype=jnp.float32) * s, 'bk': jnp.zeros((DIM,), dtype=jnp.float32), 'Wv': jax.random.normal(ks[4], (DIM, DIM), dtype=jnp.float32) * s, 'bv': jnp.zeros((DIM,), dtype=jnp.float32), 'Wo': jax.random.normal(ks[5], (DIM, DIM), dtype=jnp.float32) * s, 'bo': jnp.zeros((DIM,), dtype=jnp.float32)}
    _L0_xattn_all = _L0_xattn_setup()
    _L0_xattn_in = {k: v for k, v in _L0_xattn_all.items() if k in ('Wq', 'bq', 'Wk', 'bk', 'Wv', 'bv', 'Wo', 'bo')}
    del _L0_xattn_all

    def _L0_ffn_setup():
        import jax, jax.numpy as jnp
        import numpy as np
        DIM = 128
        HIDDEN = 384
        SCALE = 1.0 / 127.0

        def _dequant(w_int, dtype):
            return w_int.astype(dtype) * jnp.asarray(SCALE, dtype)
        key = jax.random.key(seed)
        k_x, k_g, k_u, k_d = jax.random.split(key, 4)
        x = jax.random.normal(k_x, (4, 256, DIM), dtype=jnp.float32)
        w_gate = jax.random.randint(k_g, (HIDDEN, DIM), -127, 128, dtype=jnp.int32)
        w_up = jax.random.randint(k_u, (HIDDEN, DIM), -127, 128, dtype=jnp.int32)
        w_down = jax.random.randint(k_d, (DIM, HIDDEN), -127, 128, dtype=jnp.int32)
        return {'x': x, 'w_gate': w_gate, 'w_up': w_up, 'w_down': w_down}
    _L0_ffn_all = _L0_ffn_setup()
    _L0_ffn_in = {k: v for k, v in _L0_ffn_all.items() if k in ('w_gate', 'w_up', 'w_down')}
    del _L0_ffn_all
    return {'x': x, 'ctx_1024': ctx_1024, 'g_xattn': g_xattn, 'g_ffn': g_ffn, 'L0_xattn_Wq': _L0_xattn_in['Wq'], 'L0_xattn_bq': _L0_xattn_in['bq'], 'L0_xattn_Wk': _L0_xattn_in['Wk'], 'L0_xattn_bk': _L0_xattn_in['bk'], 'L0_xattn_Wv': _L0_xattn_in['Wv'], 'L0_xattn_bv': _L0_xattn_in['bv'], 'L0_xattn_Wo': _L0_xattn_in['Wo'], 'L0_xattn_bo': _L0_xattn_in['bo'], 'L0_ffn_w_gate': _L0_ffn_in['w_gate'], 'L0_ffn_w_up': _L0_ffn_in['w_up'], 'L0_ffn_w_down': _L0_ffn_in['w_down']}

def reference(x, ctx_1024, g_xattn, g_ffn, L0_xattn_Wq, L0_xattn_bq, L0_xattn_Wk, L0_xattn_bk, L0_xattn_Wv, L0_xattn_bv, L0_xattn_Wo, L0_xattn_bo, L0_ffn_w_gate, L0_ffn_w_up, L0_ffn_w_down):
    import jax
    import jax.numpy as jnp

    def _L0_xattn_ref(x1, x2, Wq, bq, Wk, bk, Wv, bv, Wo, bo):
        import jax, jax.numpy as jnp
        import numpy as np
        DIM = 128
        N_HEADS = 16
        HEAD_DIM = DIM // N_HEADS
        B, N, M = (2, 256, 256)
        b, n, _ = x1.shape
        m = x2.shape[1]
        q = x1 @ Wq.T + bq
        k = x2 @ Wk.T + bk
        v = x2 @ Wv.T + bv
        q = q.reshape(b, n, N_HEADS, HEAD_DIM).transpose(0, 2, 1, 3)
        k = k.reshape(b, m, N_HEADS, HEAD_DIM).transpose(0, 2, 1, 3)
        v = v.reshape(b, m, N_HEADS, HEAD_DIM).transpose(0, 2, 1, 3)
        scale = 1.0 / jnp.sqrt(jnp.asarray(HEAD_DIM, dtype=q.dtype))
        scores = jnp.einsum('bhnd,bhmd->bhnm', q, k) * scale
        attn = jax.nn.softmax(scores, axis=-1)
        o = jnp.einsum('bhnm,bhmd->bhnd', attn, v)
        o = o.transpose(0, 2, 1, 3).reshape(b, n, DIM)
        return o @ Wo.T + bo

    def _L0_ffn_ref(x, w_gate, w_up, w_down):
        import jax, jax.numpy as jnp
        import numpy as np
        DIM = 128
        HIDDEN = 384
        SCALE = 1.0 / 127.0

        def _dequant(w_int, dtype):
            return w_int.astype(dtype) * jnp.asarray(SCALE, dtype)
        wg = _dequant(w_gate, x.dtype)
        wu = _dequant(w_up, x.dtype)
        wd = _dequant(w_down, x.dtype)
        gate = jnp.einsum('bsd,hd->bsh', x, wg)
        up = jnp.einsum('bsd,hd->bsh', x, wu)
        h = jax.nn.silu(gate) * up
        return jnp.einsum('bsh,dh->bsd', h, wd)
    x = x + jnp.tanh(g_xattn[0]) * _L0_xattn_ref(_layernorm(x, axis=-1), ctx_1024, L0_xattn_Wq, L0_xattn_bq, L0_xattn_Wk, L0_xattn_bk, L0_xattn_Wv, L0_xattn_bv, L0_xattn_Wo, L0_xattn_bo)
    x = x + jnp.tanh(g_ffn[0]) * _L0_ffn_ref(_layernorm(x, axis=-1), L0_ffn_w_gate, L0_ffn_w_up, L0_ffn_w_down)
    return x

_drawn_inputs = setup_inputs


def setup_inputs(seed=0):
    import zlib

    import numpy as np

    out = dict(_drawn_inputs(seed))
    spreads = {'L0_xattn_bq': (0.0, 0.31),
     'L0_xattn_bk': (0.0, 0.8),
     'L0_xattn_bv': (0.0, 0.1),
     'L0_xattn_bo': (0.0, 0.1)}
    factors = {}
    for name, (base, spread) in spreads.items():
        noise = np.random.default_rng([zlib.crc32(name.encode()), seed]).standard_normal(out[name].shape)
        drawn = base * np.exp(spread * noise) if base else spread * noise
        out[name] = jnp.asarray(drawn.astype(out[name].dtype))
    for name, factor in factors.items():
        out[name] = (out[name] * factor).astype(out[name].dtype)
    return out
```

```python
from contextlib import ExitStack

import concourse.bass as bass
from concourse import mybir

F32 = mybir.dt.float32
F32R = mybir.dt.float32r
BF16 = mybir.dt.bfloat16
I32 = mybir.dt.int32
ALU = mybir.AluOpType
ACT = mybir.ActivationFunctionType
AX = mybir.AxisListType.X

D = 128
S = 128
HD = 8
GRP = 4
HPG = 4
HEADS = GRP * HPG
ROWS = HPG * HD
NSLOT = 3
KROWS = NSLOT * ROWS
SEQ = 2
T = SEQ * S
HID_T = 3
PAIRS = HEADS // 2
VW = HD + 1
EPS = 1e-5
W_SCALE = 1.0 / 127.0
SCORE_SCALE = float(HD) ** -0.5
DMA = 16
Q_SLOTS = ("hi", "hi", "lo")
K_SLOTS = ("hi", "lo", "hi")


class Step:

    def __init__(self, i, p, blocks):
        self.i, self.p, self.blocks = i, p, blocks
        self.n = 2 * i + p

    def block(self, k):
        return 2 * self.i + (self.p + k)

    def par(self, k):
        return (self.p + k) % 2

    def half(self, k):
        return self.i + (self.p + k) // 2

    def has(self, k):
        return not isinstance(self.n, int) or 0 <= self.n + k < self.blocks


def build(nc, x, ctx_in, g_xattn, g_ffn, Wq, bq, Wk, bk, Wv, bv, Wo, bo, w_gate, w_up, w_down, out):
    NB = x.shape[0] // SEQ
    x_v = x.rearrange("(n b) t c -> n t b c", b=SEQ)
    c_v = ctx_in.rearrange("(n b) t c -> n t b c", b=SEQ)
    out_v = out.rearrange("(n b) t c -> n t b c", b=SEQ)

    with ExitStack() as stack:
        def sb(name, shape, dt=F32):
            return stack.enter_context(nc.sbuf_tensor(name, shape, dt))

        totals = {}

        def sem(name, total):
            s = stack.enter_context(nc.semaphore(name))
            totals[s] = total
            return s

        def wait(eng, s, count):
            if isinstance(count, int):
                count = min(count, totals[s])
                if count <= 0:
                    return
            eng.wait_ge(s, count)

        w_nat = sb("w_nat", [D, 4, D])
        gu_int = sb("gu_int", [D, 2, HID_T, D], I32)
        dn_int = sb("dn_int", [D, HID_T, D], I32)
        gu_nat = sb("gu_nat", [D, 2, HID_T, D])
        dn_nat = sb("dn_nat", [D, HID_T, D])
        wqT, wkT, wvT, woT = (sb(n, [D, D]) for n in ("wqT", "wkT", "wvT", "woT"))
        guT = sb("guT", [D, 2, HID_T, D])
        dnT = sb("dnT", [D, HID_T, D])
        ident = sb("ident", [D, D])
        ident_bf = sb("ident_bf", [D, D], BF16)
        head_sel = sb("head_sel", [D, HEADS, D], BF16)
        b_row = sb("b_row", [1, 2, D])
        b_row_p = sb("b_row_p", [1, 2, D])
        b_col = sb("b_col", [D, 2])
        one = sb("one", [1, 1])
        bv_col = sb("bv_col", [D, 1])
        bv_wide = sb("bv_wide", [D, D])
        bo_all = sb("bo_all", [D, D])
        gates = sb("gates", [D, 2])
        tanh_x = sb("tanh_x", [D, 1])
        tanh_f = sb("tanh_f", [D, 1])
        out_bias = sb("out_bias", [D, D])
        wait_word = sb("wait_word", [1, 1])
        neg_half = sb("neg_half", [D, SEQ])

        x_in = sb("x_in", [S, 2, SEQ, D])
        c_in = sb("c_in", [S, 2, SEQ, D])
        x_res = sb("x_res", [S, 2, SEQ, D])
        stats = sb("stats", [S, 2, SEQ, 6])
        mean_var = sb("mean_var", [S, 2, SEQ, 2])
        var_eps = sb("var_eps", [S, 2, SEQ])
        rstd = sb("rstd", [S, 2, SEQ])
        xn = sb("xn", [S, SEQ, D])
        xcT = sb("xcT", [D, 2, T])
        nat = {(w, part): sb(f"{w}_{part}", [D, T], F32R) for w in "qk" for part in ("hi", "lo")}
        plain = {w: sb(f"{w}_plain", [KROWS, 2, GRP, T], F32R) for w in "qk"}
        wide = {w: sb(f"{w}_wide", [KROWS, 2, GRP, HPG, T], F32R) for w in "qk"}
        v_ones = sb("v_ones", [S, 2, SEQ, HEADS, VW])
        neg_max = sb("neg_max", [S, 2, HEADS])
        neg_max_bf = sb("neg_max_bf", [S, 2, HEADS], BF16)
        neg_max_T = sb("neg_max_T", [D, SEQ, S], BF16)
        probs = sb("probs", [S, 2, HPG * S])
        o_raw = sb("o_raw", [D, 2, 2, S])
        o_inv = sb("o_inv", [S, 2, 2, GRP])
        o_tok = sb("o_tok", [S, D])
        oT = sb("oT", [D, S])
        x1 = sb("x1", [S, 2, SEQ, D])
        xn2 = sb("xn2", [S, SEQ, D])
        xn2T = sb("xn2T", [D, T])
        th = sb("th", [D, T])
        gated = sb("gated", [D, T])
        hT = sb("hT", [D, HID_T, T])
        x2 = sb("x2", [S, 2, SEQ, D])

        def bank(name):
            return stack.enter_context(nc.psum_tensor(name, [128, 512], F32))

        ps_a = [bank("ps_a0"), bank("ps_a1")]
        ps_b = [bank("ps_b0"), bank("ps_b1")]
        ps_o = bank("ps_o")
        ps_t = bank("ps_t")
        ps_g = bank("ps_g")
        ps_m = bank("ps_m")
        ps_t_bf = ps_t[:, :].bitcast(BF16)

        BT = NB * SEQ
        w_attn_in = sem("w_attn_in", 4 * DMA)
        w_ffn_in = sem("w_ffn_in", 3 * DMA)
        small_in = sem("small_in", 6 * DMA)
        x_loaded = [sem(f"x_loaded{i}", NB // 2 * DMA) for i in range(2)]
        c_loaded = [sem(f"c_loaded{i}", NB // 2 * DMA) for i in range(2)]
        res_loaded = [sem(f"res_loaded{i}", NB // 2 * DMA) for i in range(2)]
        PL, WD = NSLOT * GRP * DMA, HPG * DMA
        plain_landed = {w: [sem(f"{w}_plain_landed{i}", NB // 2 * PL) for i in range(2)] for w in "qk"}
        wide_landed = {w: [sem(f"{w}_wide_landed{i}", NB // 2 * WD) for i in range(2)] for w in "qk"}
        stored = [sem(f"stored{i}", NB // 2 * DMA) for i in range(2)]
        ident_set = sem("ident_set", 3)
        cleared = {"k": sem("k_cleared", 2), "q": sem("q_cleared", 2)}
        rows_set = sem("rows_set", 3)
        consts_set = sem("consts_set", 6)
        ffn_w_f32 = sem("ffn_w_f32", 2)
        tanh_ready = sem("tanh_ready", 2)
        attn_w_turned = sem("attn_w_turned", 1)
        attn_w_ready = sem("attn_w_ready", 5)
        bias_summed = sem("bias_summed", 1)
        bias_ready = sem("bias_ready", 1)
        ffn_w_turned = sem("ffn_w_turned", 1)
        gu_w_ready = sem("gu_w_ready", 2)
        dn_w_ready = sem("dn_w_ready", 1)
        a_done = sem("a_done", BT * GRP)
        b_done = sem("b_done", BT * GRP)
        av_done = sem("av_done", BT * GRP)
        max_turned = sem("max_turned", BT)
        o_turned = sem("o_turned", BT)
        otok_turned = sem("otok_turned", BT)
        proj_done = sem("proj_done", BT)
        gu_done = sem("gu_done", NB * HID_T)
        down_done = sem("down_done", BT)
        v_done = sem("v_done", NB)
        xc_turned = sem("xc_turned", NB)
        qk_done = sem("qk_done", NB)
        xn2_turned = sem("xn2_turned", NB)
        max_T_ready = sem("max_T_ready", BT)
        exp_done = sem("exp_done", BT * GRP)
        o_raw_ready = sem("o_raw_ready", BT)
        oT_ready = sem("oT_ready", BT)
        v_ready = sem("v_ready", NB)
        xcT_ready = sem("xcT_ready", NB)
        hi_ready = {w: sem(f"{w}_hi_ready", NB) for w in "qk"}
        xn2T_ready = sem("xn2T_ready", NB)
        th_ready = sem("th_ready", NB * HID_T)
        max_done = sem("max_done", BT * GRP)
        max_hi = sem("max_hi", BT)
        max_split = sem("max_split", BT)
        lo_ready = {w: sem(f"{w}_lo_ready", NB) for w in "qk"}
        stats_done = [sem("stats1_done", BT), sem("stats2_done", BT)]
        mean_var_done = [sem("mean_var1_done", BT), sem("mean_var2_done", BT)]
        var_ready = [sem("var1_ready", NB), sem("var2_ready", NB)]
        gated_done = sem("gated_done", NB * HID_T)
        h_ready = sem("h_ready", NB * HID_T)
        o_inv_done = sem("o_inv_done", 2 * BT)
        o_tok_ready = sem("o_tok_ready", 2 * BT)
        x1_ready = sem("x1_ready", BT)
        x2_ready = sem("x2_ready", BT)
        rstd_done = [sem("rstd1_done", NB), sem("rstd2_done", NB)]
        centred = [sem("centred1", NB), sem("centred2", NB)]
        xn_ready = sem("xn_ready", NB)
        xn2_ready = sem("xn2_ready", NB)
        res_ready = sem("res_ready", NB)

        def run(eng, step, first, last, loop_first, loop_last):
            for n in range(first, loop_first):
                step(Step(n // 2, n % 2, NB))
            with eng.Fori(loop_first // 2, (loop_last + 1) // 2) as i:
                for p in range(2):
                    step(Step(i, p, NB))
            for n in range(loop_last + 1, last + 1):
                step(Step(n // 2, n % 2, NB))

        FIRST, LAST = -2, NB + 1
        LOOP_FIRST, LOOP_LAST = 4, NB - 3

        block = stack.enter_context(nc.Block())

        @block.sync
        def _(sp):
            def load_inputs(st, k):
                n, p = st.block(k), st.par(k)
                wait(sp, xn_ready, n - 1)
                sp.dma_start(x_in[:, p], x_v[n]).then_inc(x_loaded[p], DMA)
                wait(sp, xc_turned, n - 1)
                sp.dma_start(c_in[:, p], c_v[n]).then_inc(c_loaded[p], DMA)

            def step(st):
                n, p = st.n, st.p
                if st.has(0):
                    wait(sp, x1_ready, SEQ * (n - 1))
                    sp.dma_start(x_res[:, p], x_v[st.block(0)]).then_inc(res_loaded[p], DMA)
                if st.has(3):
                    load_inputs(st, 3)
                if st.has(-2):
                    wait(sp, x2_ready, SEQ * (n - 1))
                    sp.dma_start(out_v[st.block(-2)], x2[:, p]).then_inc(stored[p], DMA)
                if st.has(2):
                    for w, slots in (("k", K_SLOTS), ("q", Q_SLOTS)):
                        wait(sp, a_done, 8 * (n + 1))
                        wait(sp, b_done, 8 * (n + 1))
                        wait(sp, hi_ready[w], n + 3)
                        wait(sp, lo_ready[w], n + 3)
                        for slot, part in enumerate(slots):
                            for g in range(GRP):
                                sp.dma_start(plain[w][ROWS * slot:ROWS * (slot + 1), p, g, :].bitcast(F32),
                                             nat[w, part][ROWS * g:ROWS * (g + 1), :].bitcast(F32)
                                             ).then_inc(plain_landed[w][p], DMA)
                        if isinstance(n, int) and n < 0:
                            wait(sp, cleared[w], n + 3)
                        wait(sp, plain_landed[w][p], PL * (st.half(2) + 1))
                        for j in range(HPG):
                            sp.dma_start(wide[w][j:KROWS:HPG, p, :, j, :].bitcast(F32),
                                         plain[w][j:KROWS:HPG, p, :, :].bitcast(F32)
                                         ).then_inc(wide_landed[w][p], DMA)

            load_inputs(Step(-1, 1, NB), 1)
            sp.dma_start(w_nat[:, 0, :], Wq).then_inc(w_attn_in, DMA)
            sp.dma_start(w_nat[:, 1, :], Wk).then_inc(w_attn_in, DMA)
            sp.dma_start(w_nat[:, 2, :], Wv).then_inc(w_attn_in, DMA)
            sp.dma_start(w_nat[:, 3, :], Wo).then_inc(w_attn_in, DMA)
            sp.dma_start(b_row[:, 0, :], bq.unsqueeze(0)).then_inc(small_in, DMA)
            sp.dma_start(b_row[:, 1, :], bk.unsqueeze(0)).then_inc(small_in, DMA)
            sp.dma_start(bv_col[:, :], bv.unsqueeze(1)).then_inc(small_in, DMA)
            sp.dma_start(bo_all[:, :], bo.partition_broadcast(D)).then_inc(small_in, DMA)
            sp.dma_start(gates[:, 0:1], g_xattn.partition_broadcast(D)).then_inc(small_in, DMA)
            sp.dma_start(gates[:, 1:2], g_ffn.partition_broadcast(D)).then_inc(small_in, DMA)
            sp.dma_start(gu_int[:, 0], w_gate.rearrange("(t p) d -> p t d", p=D)).then_inc(w_ffn_in, DMA)
            sp.dma_start(gu_int[:, 1], w_up.rearrange("(t p) d -> p t d", p=D)).then_inc(w_ffn_in, DMA)
            sp.dma_start(dn_int[:, :, :], w_down.rearrange("p (t d) -> p t d", t=HID_T)).then_inc(w_ffn_in, DMA)
            run(sp, step, FIRST, LAST, LOOP_FIRST, LOOP_LAST - 2)
            for p in range(2):
                sp.wait_ge(stored[p], NB // 2 * DMA)

        @block.gpsimd
        def _(pool):
            def normalise(which, src, dst, ready, n):
                wait(pool, var_ready[which], n + 1)
                pool.tensor_tensor(rstd[:, which, :], var_eps[:, which, :], neg_half[:, :],
                                   ALU.pow).then_inc(rstd_done[which], 1)
                wait(pool, rstd_done[which], n + 1)
                pool.tensor_tensor(dst[:, :, :], src,
                                   mean_var[:, which, :, 0].unsqueeze(2).to_broadcast([S, SEQ, D]),
                                   ALU.subtract).then_inc(centred[which], 1)
                wait(pool, centred[which], n + 1)
                pool.tensor_tensor(dst[:, :, :], dst[:, :, :],
                                   rstd[:, which, :].unsqueeze(2).to_broadcast([S, SEQ, D]),
                                   ALU.mult).then_inc(ready, 1)

            def step(st):
                n = st.n
                if st.has(0):
                    wait(pool, res_loaded[st.par(0)], DMA * (st.half(0) + 1))
                    pool.tensor_tensor(x_res[:, st.p], x_res[:, st.p],
                                       out_bias[:, :].unsqueeze(1).to_broadcast([S, SEQ, D]),
                                       ALU.add).then_inc(res_ready, 1)
                if st.has(2):
                    wait(pool, xc_turned, n + 2)
                    normalise(0, x_in[:, st.par(2)], xn, xn_ready, st.block(2))
                if st.has(-1):
                    wait(pool, xn2_turned, n - 1)
                    normalise(1, x1[:, st.par(-1)], xn2, xn2_ready, st.block(-1))

            pool.memset(ident[:, :], 0.0).then_inc(ident_set, 1)
            pool.wait_ge(ident_set, 1)
            pool.affine_select(out=ident[:, :], in_=ident[:, :], compare_op=ALU.not_equal, fill=1.0, base=0,
                               pattern=[[-1, D]], channel_multiplier=1).then_inc(ident_set, 1)
            pool.memset(neg_half[:, :], -0.5).then_inc(ident_set, 1)
            pool.wait_ge(ident_set, 3)
            pool.memset(wide["q"][:, 0].bitcast(F32), 0.0).then_inc(cleared["q"], 1)
            step(Step(-1, 0, NB))
            pool.memset(wide["q"][:, 1].bitcast(F32), 0.0).then_inc(cleared["q"], 1)
            step(Step(-1, 1, NB))
            pool.wait_ge(bias_ready, 1)
            run(pool, step, 0, LAST, LOOP_FIRST, LOOP_LAST)

        @block.vector
        def _(dve):
            def moments(which, src, m, used):
                wait(dve, used, m)
                for b in range(SEQ):
                    dve.bn_stats(stats[:, which, b, :], src[:, b, :]).then_inc(stats_done[which], 1)
                wait(dve, stats_done[which], SEQ * (m + 1))
                dve.memset(wait_word[:, :], 0.0)
                for b in range(SEQ):
                    dve.bn_aggr(mean_var[:, which, b, :], stats[:, which, b, :]).then_inc(mean_var_done[which], 1)
                wait(dve, mean_var_done[which], SEQ * (m + 1))
                dve.tensor_scalar(var_eps[:, which, :], mean_var[:, which, :, 1], EPS, None,
                                  ALU.add).then_inc(var_ready[which], 1)

            def step(st):
                n, p = st.n, st.p
                for u in range(8):
                    b, g = u // GRP, u % GRP

                    if st.has((b + 1) // SEQ):
                        nxt = 2 * n + b + 1
                        a = GRP * nxt + g
                        wait(dve, a_done, a + 1)
                        if g == 0:
                            wait(dve, max_split, nxt - 1)
                        dve.tensor_reduce(neg_max[:, 1 - b, g * HPG:(g + 1) * HPG],
                                          ps_a[u % 2][:, :].rearrange("p (j k) -> p j k", j=HPG),
                                          AX, ALU.max, negate=True).then_inc(max_done, 1)
                        if g == GRP - 1:
                            wait(dve, max_done, a + 1)
                            wait(dve, max_turned, nxt)
                            dve.tensor_copy(neg_max_bf[:, 0, :], neg_max[:, 1 - b, :]).then_inc(max_hi, 1)
                            wait(dve, max_hi, nxt + 1)
                            dve.tensor_tensor(neg_max_bf[:, 1, :], neg_max[:, 1 - b, :], neg_max_bf[:, 0, :],
                                              ALU.subtract).then_inc(max_split, 1)

                    if u < HID_T and st.has(-2):
                        c = HID_T * (n - 2) + u
                        wait(dve, th_ready, c + 1)
                        wait(dve, h_ready, c)
                        dve.scalar_tensor_tensor(out=gated[:, :], in0=th[:, :], scalar=1.0, in1=ps_g[:, 0:T],
                                                 op0=ALU.add, op1=ALU.mult).then_inc(gated_done, 1)
                        wait(dve, gated_done, c + 1)
                        wait(dve, down_done, SEQ * (n - 2))
                        dve.tensor_tensor(hT[:, u, :], gated[:, :], ps_g[:, T:2 * T],
                                          ALU.mult).then_inc(h_ready, 1)

                    if u == 2 and st.has(2):
                        wait(dve, x_loaded[st.par(2)], DMA * (st.half(2) + 1))
                        moments(0, x_in[:, st.par(2)], n + 2, xn_ready)

                    if g == 1 and st.has(b - 1):
                        t = 2 * n + b - 1
                        wait(dve, o_turned, t + 1)
                        wait(dve, o_tok_ready, 2 * t)
                        o_v = ps_t[:, :].rearrange("p (r i c w) -> p r i c w", r=2, i=2, c=GRP)
                        tok_v = o_tok[:, :].rearrange("p (r c i d) -> p r c i d", r=2, c=GRP, i=2)
                        for i in range(2):
                            dve.reciprocal(o_inv[:, i], o_v[:, :, i, :, VW * i + HD]).then_inc(o_inv_done, 1)
                        wait(dve, o_inv_done, 2 * t + 2)
                        wait(dve, otok_turned, t)
                        for i in range(2):
                            dve.tensor_tensor(tok_v[:, :, :, i, :], o_v[:, :, i, :, VW * i:VW * i + HD],
                                              o_inv[:, i].unsqueeze(3).to_broadcast([S, 2, GRP, HD]),
                                              ALU.mult).then_inc(o_tok_ready, 1)

                    if u == 7 and st.has(2):
                        wait(dve, hi_ready["k"], n + 3)
                        wait(dve, hi_ready["q"], n + 3)
                        for w, c in (("k", 1), ("q", 0)):
                            wait(dve, plain_landed[w][st.par(1)], PL * (st.half(1) + 1))
                            dve.scalar_tensor_tensor(out=nat[w, "lo"][:, :], in0=ps_g[:, T * c:T * (c + 1)],
                                                     scalar=b_col[:, c:c + 1],
                                                     in1=nat[w, "hi"][:, :].bitcast(F32),
                                                     op0=ALU.add, op1=ALU.subtract).then_inc(lo_ready[w], 1)

                    if g == 3 and st.has(b - 1):
                        t = 2 * n + b - 1
                        pt, bt = st.par(b - 1), 1 - b
                        wait(dve, proj_done, t + 1)
                        wait(dve, res_ready, st.block(b - 1) + 1)
                        wait(dve, x2_ready, t - 3)
                        dve.tensor_tensor(x1[:, pt, bt, :], ps_m[:, 0:D], x_res[:, pt, bt, :],
                                          ALU.add).then_inc(x1_ready, 1)

                    if u == 4 and st.has(-1):
                        wait(dve, x1_ready, SEQ * n)
                        moments(1, x1[:, st.par(-1)], n - 1, xn2_ready)

                    if u in (4, 5) and st.has(-2):
                        s = u - 4
                        wait(dve, down_done, SEQ * (n - 2) + s + 1)
                        wait(dve, stored[p], DMA * st.half(-2))
                        dve.tensor_tensor(x2[:, p, s, :], ps_m[:, 0:D], x1[:, p, s, :],
                                          ALU.add).then_inc(x2_ready, 1)

            dve.memset(one[:, :], 1.0).then_inc(consts_set, 1)
            dve.memset(ps_o[:, :], 0.0).then_inc(consts_set, 1)
            dve.memset(v_ones[:, :, :, :, :], 1.0).then_inc(consts_set, 1)
            dve.memset(neg_max_T[:, :, :], 0.0).then_inc(consts_set, 1)
            dve.wait_ge(ident_set, 2)
            dve.tensor_copy(ident_bf[:, :], ident[:, :]).then_inc(consts_set, 1)
            dve.wait_ge(consts_set, 5)
            dve.tensor_tensor(head_sel[:, :, :], ident_bf[:, 0:HEADS].unsqueeze(2).to_broadcast([D, HEADS, D]),
                              ident_bf[:, HEADS:2 * HEADS].unsqueeze(2).to_broadcast([D, HEADS, D]),
                              ALU.add).then_inc(consts_set, 1)
            dve.wait_ge(small_in, 6 * DMA)
            for w in range(2):
                dve.tensor_copy(b_row_p[:, w, :].rearrange("p (g d j) -> p g j d", g=GRP, d=HD),
                                b_row[:, w, :].rearrange("p (g j d) -> p g j d", g=GRP, d=HD)
                                ).then_inc(rows_set, 1)
            dve.tensor_copy(bv_wide[:, :], bv_col[:, 0:1].to_broadcast([D, D])).then_inc(rows_set, 1)
            dve.memset(wide["k"][:, 0].bitcast(F32), 0.0).then_inc(cleared["k"], 1)

            dve.wait_ge(attn_w_turned, 1)
            dve.wait_ge(tanh_ready, 2)
            for w, wT in enumerate((wqT, wkT)):
                dve.tensor_copy(wT[:, :].rearrange("p (g d j) -> p g j d", g=GRP, d=HD),
                                ps_g[:, D * w:D * (w + 1)].rearrange("p (g j d) -> p g j d", g=GRP, d=HD)
                                ).then_inc(attn_w_ready, 1)
            dve.tensor_copy(wvT[:, :], ps_g[:, 2 * D:3 * D]).then_inc(attn_w_ready, 1)
            dve.tensor_scalar(woT[:, :], ps_g[:, 3 * D:4 * D], tanh_x[:, :], None, ALU.mult).then_inc(attn_w_ready, 1)
            dve.tensor_copy(b_col[:, :], ps_m[:, 0:2]).then_inc(attn_w_ready, 1)
            dve.wait_ge(bias_summed, 1)
            dve.scalar_tensor_tensor(out=out_bias[:, :], in0=bo_all[:, :], scalar=tanh_x[:, :], in1=ps_a[0][:, 0:D],
                                     op0=ALU.mult, op1=ALU.add).then_inc(bias_ready, 1)
            step(Step(-1, 0, NB))
            dve.wait_ge(ffn_w_turned, 1)
            dve.tensor_scalar(dnT[:, :, :], ps_t[:, 0:HID_T * D].rearrange("p (t d) -> p t d", t=HID_T),
                              tanh_f[:, :], 0.5, ALU.mult, ALU.mult).then_inc(dn_w_ready, 1)
            dve.memset(wide["k"][:, 1].bitcast(F32), 0.0).then_inc(cleared["k"], 1)
            run(dve, step, -1, LAST, LOOP_FIRST, LOOP_LAST)

        @block.scalar
        def _(act):
            def step(st):
                n, p = st.n, st.p
                for u in range(8):
                    b, g = u // GRP, u % GRP
                    seq = 2 * n + b
                    slot = GRP * seq + g
                    t = seq - 1

                    if g == 0 and st.has(0):
                        wait(act, max_turned, seq + 1)
                        wait(act, b_done, GRP * (seq - 1))
                        act.copy(neg_max_T[0:2 * HEADS, b, :], ps_t_bf[0:2 * HEADS, 0:S]).then_inc(max_T_ready, 1)
                    if g == 1 and st.has(b - 1):
                        wait(act, av_done, GRP * (t + 1))
                        wait(act, o_turned, t)
                        act.copy(o_raw[:, :, :, :], ps_o[:, :].rearrange("p (r i q) -> p r i q", r=2, i=2)
                                 ).then_inc(o_raw_ready, 1)
                    if u < HID_T and st.has(-2):
                        c = HID_T * (n - 2) + u
                        wait(act, gu_done, c + 1)
                        wait(act, gated_done, c)
                        act.activation(th[:, :], ps_g[:, 0:T], ACT.Tanh, scale=0.5).then_inc(th_ready, 1)
                    if g == 2 and st.has(b - 1):
                        wait(act, otok_turned, t + 1)
                        wait(act, proj_done, t)
                        act.copy(oT[:, :], ps_t[:, 0:S]).then_inc(oT_ready, 1)
                    if u == 3 and st.has(1):
                        wait(act, v_done, n + 2)
                        wait(act, av_done, 8 * n)
                        act.copy(v_ones[:, st.par(1), :, :, 0:HD],
                                 ps_g[:, 0:T].rearrange("p (b h d) -> p b h d", b=SEQ, h=HEADS)
                                 ).then_inc(v_ready, 1)
                    if u == 6 and st.has(2):
                        wait(act, xc_turned, n + 3)
                        wait(act, v_done, n + 2)
                        wait(act, qk_done, n + 2)
                        act.copy(xcT[:, :, :], ps_g[:, :].rearrange("p (w t) -> p w t", w=2)).then_inc(xcT_ready, 1)
                    if u == 7 and st.has(2):
                        wait(act, qk_done, n + 3)
                        for w, c in (("k", 1), ("q", 0)):
                            wait(act, plain_landed[w][st.par(1)], PL * (st.half(1) + 1))
                            act.activation(nat[w, "hi"][:, :], ps_g[:, T * c:T * (c + 1)], ACT.Identity,
                                           bias=b_col[:, c:c + 1]).then_inc(hi_ready[w], 1)
                    if u == 7 and st.has(-1):
                        wait(act, xn2_turned, n)
                        wait(act, gu_done, HID_T * (n - 1))
                        act.copy(xn2T[:, :], ps_t[:, 0:T]).then_inc(xn2T_ready, 1)
                    if st.has(0):
                        wait(act, b_done, slot + 1)
                        wait(act, av_done, slot - 1)
                        act.activation(probs[:, u % 2, :], ps_b[u % 2][:, :], ACT.Exp,
                                       scale=SCORE_SCALE).then_inc(exp_done, 1)

            act.wait_ge(small_in, 6 * DMA)
            act.activation(tanh_x[:, :], gates[:, 0:1], ACT.Tanh).then_inc(tanh_ready, 1)
            act.activation(tanh_f[:, :], gates[:, 1:2], ACT.Tanh).then_inc(tanh_ready, 1)
            act.wait_ge(w_ffn_in, 3 * DMA)
            act.activation(gu_nat[:, :, :, :], gu_int[:, :, :, :], ACT.Copy, scale=W_SCALE).then_inc(ffn_w_f32, 1)
            act.activation(dn_nat[:, :, :], dn_int[:, :, :], ACT.Copy, scale=W_SCALE).then_inc(ffn_w_f32, 1)
            act.wait_ge(consts_set, 6)
            act.wait_ge(attn_w_ready, 5)
            step(Step(-1, 0, NB))
            act.wait_ge(ffn_w_turned, 1)
            for w in range(2):
                act.copy(guT[:, w, :, :], ps_b[w][:, 0:HID_T * D].rearrange("p (t d) -> p t d", t=HID_T)
                         ).then_inc(gu_w_ready, 1)
            run(act, step, -1, LAST, LOOP_FIRST, LOOP_LAST)

        @block.tensor
        def _(pe):
            def values(n, b, g, par):
                seq = SEQ * n + b
                wait(pe, exp_done, GRP * seq + g + 1)
                if g == 0:
                    wait(pe, o_raw_ready, seq)
                    wait(pe, v_ready, n + 1)
                for jj in range(2):
                    pair = 2 * g + jj
                    r, c = pair // GRP, pair % GRP
                    mm = pe.matmul(ps_o[32 * c:32 * c + 2 * VW, r * 2 * S:(r + 1) * 2 * S],
                                   v_ones[:, par, b, 2 * pair:2 * pair + 2, :],
                                   probs[:, g % 2, jj * 2 * S:(jj + 1) * 2 * S], start=True, stop=True)
                mm.then_inc(av_done, 1)

            def step(st):
                n, p = st.n, st.p
                for u in range(8):
                    b, g = u // GRP, u % GRP
                    seq = 2 * n + b
                    slot = GRP * seq + g
                    t = seq - 1

                    kb = (b + 1) // SEQ
                    if st.has(kb):
                        a = slot + GRP
                        nb, pp = 1 - b, st.par(kb)
                        if u == GRP:
                            wait(pe, plain_landed["q"][pp], PL * (st.half(kb) + 1))
                            wait(pe, wide_landed["k"][pp], WD * (st.half(kb) + 1))
                        wait(pe, max_done, a - 1)
                        pe.matmul(ps_a[u % 2][:, :], plain["q"][:, pp, g, nb * S:(nb + 1) * S],
                                  wide["k"][:, pp, g, :, nb * S:(nb + 1) * S],
                                  start=True, stop=True).then_inc(a_done, 1)

                    if st.has(0):
                        if u == 0:
                            wait(pe, plain_landed["k"][p], PL * (st.half(0) + 1))
                            wait(pe, wide_landed["q"][p], WD * (st.half(0) + 1))
                        wait(pe, exp_done, slot - 1)
                        pe.matmul(ps_b[u % 2][:, :], plain["k"][:, p, g, b * S:(b + 1) * S],
                                  wide["q"][:, p, g, :, b * S:(b + 1) * S],
                                  start=True, stop=False, skip_group_check=True)
                        if g == 0:
                            wait(pe, max_split, seq + 1)
                            wait(pe, xn2T_ready, n - 1)
                            wait(pe, oT_ready, 2 * n - 1 + b)
                            pe.transpose(ps_t_bf[0:2 * HEADS, 0:S],
                                         neg_max_bf[:, :, :].rearrange("p w h -> p (w h)"),
                                         ident_bf[:, :]).then_inc(max_turned, 1)

                    if u < HID_T and st.has(-2):
                        c = HID_T * (n - 2) + u
                        wait(pe, xn2T_ready, n - 1)
                        wait(pe, lo_ready["q"], n + 2)
                        wait(pe, h_ready, c)
                        for w in range(2):
                            mm = pe.matmul(ps_g[:, T * w:T * (w + 1)], guT[:, w, u, :], xn2T[:, :],
                                           start=True, stop=True)
                        mm.then_inc(gu_done, 1)

                    if u == 3 and st.has(1):
                        wait(pe, xcT_ready, n + 2)
                        wait(pe, lo_ready["q"], n + 2)
                        wait(pe, h_ready, HID_T * (n - 1))
                        for s in range(SEQ):
                            mm = pe.matmul(ps_g[:, D * s:D * (s + 1)], xcT[:, 1, S * s:S * (s + 1)], wvT[:, :],
                                           start=True, stop=True)
                        mm.then_inc(v_done, 1)

                    if u in (4, 5) and st.has(-2):
                        s = u - 4
                        wait(pe, h_ready, HID_T * (n - 1))
                        wait(pe, x1_ready, SEQ * n)
                        wait(pe, x2_ready, SEQ * (n - 2) + s)
                        for c in range(HID_T):
                            mm = pe.matmul(ps_m[:, 0:D], hT[:, c, S * s:S * (s + 1)], dnT[:, c, :],
                                           start=(c == 0), stop=(c == HID_T - 1))
                        mm.then_inc(down_done, 1)

                    if g == 1 and st.has(b - 1):
                        wait(pe, o_raw_ready, t + 1)
                        wait(pe, max_T_ready, seq + 1)
                        for r in range(2):
                            for i in range(2):
                                mm = pe.transpose(ps_t[:, (2 * r + i) * S:(2 * r + i + 1) * S], o_raw[:, r, i, :],
                                                  ident[:, :])
                        mm.then_inc(o_turned, 1)

                    if g == 2 and st.has(b - 1):
                        wait(pe, o_tok_ready, 2 * (t + 1))
                        pe.transpose(ps_t[:, 0:S], o_tok[:, :], ident[:, :]).then_inc(otok_turned, 1)

                    if u == 6 and st.has(2):
                        wait(pe, xn_ready, n + 3)
                        wait(pe, c_loaded[st.par(2)], DMA * (st.half(2) + 1))
                        wait(pe, v_ready, n + 2)
                        wait(pe, h_ready, HID_T * (n - 1))
                        for s in range(SEQ):
                            pe.transpose(ps_g[:, S * s:S * (s + 1)], xn[:, s, :], ident[:, :])
                            mm = pe.transpose(ps_g[:, T + S * s:T + S * (s + 1)], c_in[:, st.par(2), s, :],
                                              ident[:, :])
                        mm.then_inc(xc_turned, 1)

                    if g == 3 and st.has(b - 1):
                        wait(pe, oT_ready, t + 1)
                        wait(pe, x1_ready, t)
                        wait(pe, x2_ready, SEQ * (n - 2 + b))
                        pe.matmul(ps_m[:, 0:D], oT[:, :], woT[:, :], start=True, stop=True).then_inc(proj_done, 1)

                    if u == 7 and st.has(2):
                        wait(pe, xcT_ready, n + 3)
                        pe.matmul(ps_g[:, 0:T], wqT[:, :], xcT[:, 0, :], start=True, stop=True)
                        pe.matmul(ps_g[:, T:2 * T], wkT[:, :], xcT[:, 1, :], start=True, stop=True
                                  ).then_inc(qk_done, 1)

                    if u == 7 and st.has(-1):
                        wait(pe, xn2_ready, n)
                        wait(pe, oT_ready, 2 * n + 1)
                        for s in range(SEQ):
                            mm = pe.transpose(ps_t[:, S * s:S * (s + 1)], xn2[:, s, :], ident[:, :])
                        mm.then_inc(xn2_turned, 1)

                    if u == 0 and st.has(-1):
                        values(n - 1, 1, GRP - 1, st.par(-1))
                    elif u > 0 and st.has(0):
                        values(n, (u - 1) // GRP, (u - 1) % GRP, p)

                    if st.has(0):
                        wait(pe, max_T_ready, seq + 1)
                        for j in range(HPG):
                            mm = pe.matmul(ps_b[u % 2][:, S * j:S * (j + 1)], head_sel[:, HPG * g + j, :],
                                           neg_max_T[:, b, :], start=False, stop=(j == HPG - 1),
                                           skip_group_check=True)
                        mm.then_inc(b_done, 1)

            pe.wait_ge(ident_set, 2)
            pe.wait_ge(w_attn_in, 4 * DMA)
            for w in range(4):
                pe.transpose(ps_g[:, D * w:D * (w + 1)], w_nat[:, w, :], ident[:, :])
            pe.wait_ge(rows_set, 3)
            pe.wait_ge(consts_set, 6)
            for w in range(2):
                mm = pe.matmul(ps_m[:, w:w + 1], b_row_p[0:1, w, :], one[0:1, 0:1], start=True, stop=True)
            mm.then_inc(attn_w_turned, 1)
            pe.wait_ge(attn_w_ready, 5)
            pe.matmul(ps_a[0][:, 0:D], bv_wide[:, :], woT[:, :], start=True, stop=True).then_inc(bias_summed, 1)
            step(Step(-1, 0, NB))
            pe.wait_ge(ffn_w_f32, 2)
            for t in range(HID_T):
                for w in range(2):
                    pe.transpose(ps_b[w][:, D * t:D * (t + 1)], gu_nat[:, w, t, :], ident[:, :])
                mm = pe.transpose(ps_t[:, D * t:D * (t + 1)], dn_nat[:, t, :], ident[:, :])
            mm.then_inc(ffn_w_turned, 1)
            pe.wait_ge(bias_ready, 1)
            step(Step(-1, 1, NB))
            pe.wait_ge(gu_w_ready, 2)
            pe.wait_ge(dn_w_ready, 1)
            run(pe, step, 0, LAST, LOOP_FIRST, LOOP_LAST)


INPUTS = ["x", "ctx_1024", "g_xattn", "g_ffn", "L0_xattn_Wq", "L0_xattn_bq", "L0_xattn_Wk", "L0_xattn_bk",
          "L0_xattn_Wv", "L0_xattn_bv", "L0_xattn_Wo", "L0_xattn_bo", "L0_ffn_w_gate", "L0_ffn_w_up",
          "L0_ffn_w_down"]


def kernel(**inputs):
    import numpy as np
    import concourse.bacc as bacc
    from concourse.bass_utils import run_bass_kernel_spmd

    nc = bacc.Bacc("TRN2", target_bir_lowering=False, num_devices=1)
    arrays, args = {}, []
    for name in INPUTS:
        a = np.ascontiguousarray(inputs[name])
        arrays[f"in_{name}"] = a
        args.append(nc.dram_tensor(f"in_{name}", a.shape, mybir.dt.from_np(a.dtype), kind="ExternalInput").ap())
    shape = arrays["in_x"].shape
    out = nc.dram_tensor("out_x", shape, F32, kind="ExternalOutput").ap()
    build(nc, *args, out)
    result = run_bass_kernel_spmd(nc, [arrays], core_ids=[0])
    return result.results[0]["out_x"]
```

```python
from contextlib import ExitStack

import concourse.bass as bass
from concourse import mybir

F32 = mybir.dt.float32
F32R = mybir.dt.float32r
BF16 = mybir.dt.bfloat16
I32 = mybir.dt.int32
ALU = mybir.AluOpType
ACT = mybir.ActivationFunctionType
AX = mybir.AxisListType.X

D = 128
S = 128
HD = 8
GRP = 4
HPG = 4
HEADS = GRP * HPG
ROWS = HPG * HD
NSLOT = 3
KROWS = NSLOT * ROWS
SEQ = 2
T = SEQ * S
HID_T = 3
PAIRS = HEADS // 2
VW = HD + 1
EPS = 1e-5
W_SCALE = 1.0 / 127.0
LEAD = 5
SCORE_SCALE = float(HD) ** -0.5
DMA = 16
HI = 0
LO = {"q": 2, "k": 1}
COPY = {"q": 1, "k": 2}


class Step:

    def __init__(self, i, p, blocks):
        self.i, self.p, self.blocks = i, p, blocks
        self.n = 2 * i + p

    def block(self, k):
        return 2 * self.i + (self.p + k)

    def par(self, k):
        return (self.p + k) % 2

    def half(self, k):
        return self.i + (self.p + k) // 2

    def has(self, k):
        return not isinstance(self.n, int) or 0 <= self.n + k < self.blocks


def build(nc, x, ctx_in, g_xattn, g_ffn, Wq, bq, Wk, bk, Wv, bv, Wo, bo, w_gate, w_up, w_down, out):
    NB = x.shape[0] // SEQ
    x_v = x.rearrange("(n b) t c -> n t b c", b=SEQ)
    c_v = ctx_in.rearrange("(n b) t c -> n t b c", b=SEQ)
    out_v = out.rearrange("(n b) t c -> n t b c", b=SEQ)

    with ExitStack() as stack:
        def sb(name, shape, dt=F32):
            return stack.enter_context(nc.sbuf_tensor(name, shape, dt))

        totals = {}

        def sem(name, total):
            s = stack.enter_context(nc.semaphore(name))
            totals[s] = total
            return s

        def wait(eng, s, count):
            if isinstance(count, int):
                count = min(count, totals[s])
                if count <= 0:
                    return
            eng.wait_ge(s, count)

        w_nat = sb("w_nat", [D, 4, D])
        gu_int = sb("gu_int", [D, 2, HID_T, D], I32)
        dn_int = sb("dn_int", [D, HID_T, D], I32)
        gu_nat = sb("gu_nat", [D, 2, HID_T, D])
        dn_nat = sb("dn_nat", [D, HID_T, D])
        wqT, wkT, wvT, woT = (sb(n, [D, D]) for n in ("wqT", "wkT", "wvT", "woT"))
        guT = sb("guT", [D, 2, HID_T, D])
        dnT = sb("dnT", [D, HID_T, D])
        ident = sb("ident", [D, D])
        ident_bf = sb("ident_bf", [D, D], BF16)
        head_sel = sb("head_sel", [D, HEADS, D], BF16)
        b_row = sb("b_row", [1, 2, D])
        b_row_p = sb("b_row_p", [1, 2, D])
        b_col = sb("b_col", [D, 2])
        b_grp = sb("b_grp", [ROWS, 2, GRP])
        one = sb("one", [1, 1])
        bv_col = sb("bv_col", [D, 1])
        bv_wide = sb("bv_wide", [D, D])
        bo_all = sb("bo_all", [D, D])
        gates = sb("gates", [D, 2])
        tanh_x = sb("tanh_x", [D, 1])
        tanh_f = sb("tanh_f", [D, 1])
        out_bias = sb("out_bias", [D, D])
        wait_word = sb("wait_word", [1, 1])
        neg_half = sb("neg_half", [D, SEQ])

        x_in = sb("x_in", [S, 2, SEQ, D])
        c_in = sb("c_in", [S, 2, SEQ, D])
        x_res = sb("x_res", [S, 2, SEQ, D])
        stats = sb("stats", [S, 2, SEQ, 6])
        mean_var = sb("mean_var", [S, 2, SEQ, 2])
        var_eps = sb("var_eps", [S, 2, SEQ])
        rstd = sb("rstd", [S, 2, SEQ])
        xn = sb("xn", [S, SEQ, D])
        xcT = sb("xcT", [D, 2, T])
        k_new = sb("k_new", [KROWS, GRP, T], F32R)
        plain = {w: sb(f"{w}_plain", [KROWS, 2, GRP, T], F32R) for w in "qk"}
        wide = {w: sb(f"{w}_wide", [KROWS, 2, GRP, HPG, T], F32R) for w in "qk"}
        v_ones = sb("v_ones", [S, 2, SEQ, HEADS, VW])
        neg_max = sb("neg_max", [S, 2, HEADS])
        neg_max_bf = sb("neg_max_bf", [S, 2, HEADS], BF16)
        neg_max_T = sb("neg_max_T", [D, SEQ, S], BF16)
        probs = sb("probs", [S, 2, HPG * S])
        o_raw = sb("o_raw", [D, 2, 2, S])
        o_inv = sb("o_inv", [S, 2, 2, GRP])
        o_tok = sb("o_tok", [S, D])
        oT = sb("oT", [D, S])
        x1 = sb("x1", [S, 2, SEQ, D])
        xn2 = sb("xn2", [S, SEQ, D])
        xn2T = sb("xn2T", [D, T])
        th = sb("th", [D, T])
        gated = sb("gated", [D, T])
        hT = sb("hT", [D, HID_T, T])
        x2 = sb("x2", [S, 2, SEQ, D])

        def bank(name):
            return stack.enter_context(nc.psum_tensor(name, [128, 512], F32))

        ps_a = bank("ps_a")
        ps_b = [bank("ps_b0"), bank("ps_b1")]
        ps_o = bank("ps_o")
        ps_t = bank("ps_t")
        ps_g = [bank("ps_g0"), bank("ps_g1")]
        ps_m = bank("ps_m")
        ffn_bank = [ps_m, ps_g[0], ps_g[1]]
        ps_t_bf = ps_t[:, :].bitcast(BF16)

        BT = NB * SEQ
        w_attn_in = sem("w_attn_in", 4 * DMA)
        w_ffn_in = sem("w_ffn_in", 3 * DMA)
        small_in = sem("small_in", 6 * DMA)
        x_loaded = [sem(f"x_loaded{i}", NB // 2 * DMA) for i in range(2)]
        c_loaded = [sem(f"c_loaded{i}", NB // 2 * DMA) for i in range(2)]
        res_loaded = [sem(f"res_loaded{i}", NB // 2 * DMA) for i in range(2)]
        WD = HPG * DMA
        k_copied = sem("k_copied", NB * DMA)
        plain_landed = {w: [sem(f"{w}_plain_landed{i}", NB // 2 * DMA) for i in range(2)] for w in "qk"}
        wide_landed = {w: [sem(f"{w}_wide_landed{i}", NB // 2 * WD) for i in range(2)] for w in "qk"}
        stored = [sem(f"stored{i}", NB // 2 * DMA) for i in range(2)]
        ident_set = sem("ident_set", 3)
        cleared = {"k": sem("k_cleared", 2), "q": sem("q_cleared", 2)}
        rows_set = sem("rows_set", 3)
        consts_set = sem("consts_set", 6)
        ffn_w_f32 = sem("ffn_w_f32", 2)
        tanh_ready = sem("tanh_ready", 2)
        attn_w_turned = sem("attn_w_turned", 1)
        attn_w_ready = sem("attn_w_ready", 6)
        bias_summed = sem("bias_summed", 1)
        bias_ready = sem("bias_ready", 1)
        ffn_w_turned = sem("ffn_w_turned", 1)
        gu_w_ready = sem("gu_w_ready", 2)
        dn_w_ready = sem("dn_w_ready", 1)
        a_done = sem("a_done", BT * GRP)
        b_done = sem("b_done", BT * GRP)
        av_done = sem("av_done", BT * GRP)
        max_turned = sem("max_turned", BT)
        o_turned = sem("o_turned", BT)
        otok_turned = sem("otok_turned", BT)
        proj_done = sem("proj_done", BT)
        gu_done = sem("gu_done", NB * HID_T)
        down_done = sem("down_done", BT)
        v_done = sem("v_done", NB)
        xc_turned = sem("xc_turned", NB)
        k_done = sem("k_done", NB)
        q_done = sem("q_done", NB)
        xn2_turned = sem("xn2_turned", NB)
        max_T_ready = sem("max_T_ready", BT)
        exp_done = sem("exp_done", BT * GRP)
        o_raw_ready = sem("o_raw_ready", BT)
        oT_ready = sem("oT_ready", BT)
        v_ready = sem("v_ready", NB)
        xcT_ready = sem("xcT_ready", NB)
        hi_ready = {w: sem(f"{w}_hi_ready", NB * GRP) for w in "qk"}
        xn2T_ready = sem("xn2T_ready", NB)
        th_ready = sem("th_ready", NB * HID_T)
        max_done = sem("max_done", BT * GRP)
        max_hi = sem("max_hi", BT)
        max_split = sem("max_split", BT)
        lo_ready = {w: sem(f"{w}_lo_ready", NB * GRP) for w in "qk"}
        stats_done = [sem("stats1_done", BT), sem("stats2_done", BT)]
        mean_var_done = [sem("mean_var1_done", BT), sem("mean_var2_done", BT)]
        var_ready = [sem("var1_ready", NB), sem("var2_ready", NB)]
        gated_done = sem("gated_done", NB * HID_T)
        h_ready = sem("h_ready", NB * HID_T)
        o_inv_done = sem("o_inv_done", 2 * BT)
        o_tok_ready = sem("o_tok_ready", 2 * BT)
        x1_ready = sem("x1_ready", BT)
        x2_ready = sem("x2_ready", BT)
        rstd_done = [sem("rstd1_done", NB), sem("rstd2_done", NB)]
        centred = [sem("centred1", NB), sem("centred2", NB)]
        xn_ready = sem("xn_ready", NB)
        xn2_ready = sem("xn2_ready", NB)
        res_ready = sem("res_ready", NB)

        def run(eng, step, first, last, loop_first, loop_last):
            for n in range(first, loop_first):
                step(Step(n // 2, n % 2, NB))
            with eng.Fori(loop_first // 2, (loop_last + 1) // 2) as i:
                for p in range(2):
                    step(Step(i, p, NB))
            for n in range(loop_last + 1, last + 1):
                step(Step(n // 2, n % 2, NB))

        FIRST, LAST = -2, NB + 1
        LOOP_FIRST, LOOP_LAST = 4, NB - 3

        block = stack.enter_context(nc.Block())

        @block.sync
        def _(sp):
            def load_inputs(st, k):
                n, p = st.block(k), st.par(k)
                wait(sp, xn_ready, n - 1)
                sp.dma_start(x_in[:, p], x_v[n]).then_inc(x_loaded[p], DMA)
                wait(sp, xc_turned, n - 1)
                sp.dma_start(c_in[:, p], c_v[n]).then_inc(c_loaded[p], DMA)

            def step(st):
                n, p = st.n, st.p
                if st.has(0):
                    wait(sp, x1_ready, SEQ * (n - 1))
                    sp.dma_start(x_res[:, p], x_v[st.block(0)]).then_inc(res_loaded[p], DMA)
                if st.has(3):
                    load_inputs(st, 3)
                if st.has(-2):
                    wait(sp, x2_ready, SEQ * (n - 1))
                    sp.dma_start(out_v[st.block(-2)], x2[:, p]).then_inc(stored[p], DMA)
                if st.has(2):
                    def widen(w, src):
                        if isinstance(n, int) and n < 0:
                            wait(sp, cleared[w], n + 3)
                        for j in range(HPG):
                            sp.dma_start(wide[w][j:KROWS:HPG, p, :, j, :].bitcast(F32),
                                         src[j:KROWS:HPG].bitcast(F32)).then_inc(wide_landed[w][p], DMA)

                    def copy_slot(w, tile, landed):
                        sp.dma_start(tile[ROWS * COPY[w]:ROWS * (COPY[w] + 1)].bitcast(F32),
                                     tile[0:ROWS].bitcast(F32)).then_inc(landed, DMA)

                    wait(sp, lo_ready["k"], GRP * (n + 3))
                    copy_slot("k", k_new, k_copied)
                    wait(sp, k_copied, DMA * (n + 3))
                    widen("k", k_new[:, :, :])
                    wait(sp, lo_ready["q"], GRP * (n + 3))
                    copy_slot("q", plain["q"][:, p], plain_landed["q"][p])
                    wait(sp, b_done, 8 * (n + 1))
                    sp.dma_start(plain["k"][:, p].bitcast(F32), k_new[:, :, :].bitcast(F32)
                                 ).then_inc(plain_landed["k"][p], DMA)
                    wait(sp, plain_landed["q"][p], DMA * (st.half(2) + 1))
                    widen("q", plain["q"][:, p])

            load_inputs(Step(-1, 1, NB), 1)
            sp.dma_start(w_nat[:, 0, :], Wq).then_inc(w_attn_in, DMA)
            sp.dma_start(w_nat[:, 1, :], Wk).then_inc(w_attn_in, DMA)
            sp.dma_start(w_nat[:, 2, :], Wv).then_inc(w_attn_in, DMA)
            sp.dma_start(w_nat[:, 3, :], Wo).then_inc(w_attn_in, DMA)
            sp.dma_start(b_row[:, 0, :], bq.unsqueeze(0)).then_inc(small_in, DMA)
            sp.dma_start(b_row[:, 1, :], bk.unsqueeze(0)).then_inc(small_in, DMA)
            sp.dma_start(bv_col[:, :], bv.unsqueeze(1)).then_inc(small_in, DMA)
            sp.dma_start(bo_all[:, :], bo.partition_broadcast(D)).then_inc(small_in, DMA)
            sp.dma_start(gates[:, 0:1], g_xattn.partition_broadcast(D)).then_inc(small_in, DMA)
            sp.dma_start(gates[:, 1:2], g_ffn.partition_broadcast(D)).then_inc(small_in, DMA)
            sp.dma_start(gu_int[:, 0], w_gate.rearrange("(t p) d -> p t d", p=D)).then_inc(w_ffn_in, DMA)
            sp.dma_start(gu_int[:, 1], w_up.rearrange("(t p) d -> p t d", p=D)).then_inc(w_ffn_in, DMA)
            sp.dma_start(dn_int[:, :, :], w_down.rearrange("p (t d) -> p t d", t=HID_T)).then_inc(w_ffn_in, DMA)
            run(sp, step, FIRST, LAST, LOOP_FIRST, LOOP_LAST - 2)
            for p in range(2):
                sp.wait_ge(stored[p], NB // 2 * DMA)

        @block.gpsimd
        def _(pool):
            def normalise(which, src, dst, ready, n):
                wait(pool, var_ready[which], n + 1)
                pool.tensor_tensor(rstd[:, which, :], var_eps[:, which, :], neg_half[:, :],
                                   ALU.pow).then_inc(rstd_done[which], 1)
                wait(pool, rstd_done[which], n + 1)
                pool.tensor_tensor(dst[:, :, :], src,
                                   mean_var[:, which, :, 0].unsqueeze(2).to_broadcast([S, SEQ, D]),
                                   ALU.subtract).then_inc(centred[which], 1)
                wait(pool, centred[which], n + 1)
                pool.tensor_tensor(dst[:, :, :], dst[:, :, :],
                                   rstd[:, which, :].unsqueeze(2).to_broadcast([S, SEQ, D]),
                                   ALU.mult).then_inc(ready, 1)

            def step(st):
                n = st.n
                if st.has(2):
                    wait(pool, xc_turned, n + 2)
                    normalise(0, x_in[:, st.par(2)], xn, xn_ready, st.block(2))
                if st.has(0):
                    wait(pool, res_loaded[st.par(0)], DMA * (st.half(0) + 1))
                    pool.tensor_tensor(x_res[:, st.p], x_res[:, st.p],
                                       out_bias[:, :].unsqueeze(1).to_broadcast([S, SEQ, D]),
                                       ALU.add).then_inc(res_ready, 1)
                if st.has(-1):
                    wait(pool, xn2_turned, n - 1)
                    normalise(1, x1[:, st.par(-1)], xn2, xn2_ready, st.block(-1))

            pool.memset(ident[:, :], 0.0).then_inc(ident_set, 1)
            pool.wait_ge(ident_set, 1)
            pool.affine_select(out=ident[:, :], in_=ident[:, :], compare_op=ALU.not_equal, fill=1.0, base=0,
                               pattern=[[-1, D]], channel_multiplier=1).then_inc(ident_set, 1)
            pool.memset(neg_half[:, :], -0.5).then_inc(ident_set, 1)
            pool.wait_ge(ident_set, 3)
            pool.memset(wide["q"][:, 0].bitcast(F32), 0.0).then_inc(cleared["q"], 1)
            step(Step(-1, 0, NB))
            pool.memset(wide["q"][:, 1].bitcast(F32), 0.0).then_inc(cleared["q"], 1)
            step(Step(-1, 1, NB))
            pool.wait_ge(bias_ready, 1)
            run(pool, step, 0, LAST, LOOP_FIRST, LOOP_LAST)

        @block.vector
        def _(dve):
            def moments(which, src, m, used):
                wait(dve, used, m)
                for b in range(SEQ):
                    dve.bn_stats(stats[:, which, b, :], src[:, b, :]).then_inc(stats_done[which], 1)
                wait(dve, stats_done[which], SEQ * (m + 1))
                dve.memset(wait_word[:, :], 0.0)
                for b in range(SEQ):
                    dve.bn_aggr(mean_var[:, which, b, :], stats[:, which, b, :]).then_inc(mean_var_done[which], 1)
                wait(dve, mean_var_done[which], SEQ * (m + 1))
                dve.tensor_scalar(var_eps[:, which, :], mean_var[:, which, :, 1], EPS, None,
                                  ALU.add).then_inc(var_ready[which], 1)

            def step(st):
                n, p = st.n, st.p
                for u in range(8):
                    b, g = u // GRP, u % GRP

                    if st.has((u + LEAD) // 8):
                        ahead, ga = (u + LEAD) // GRP, (u + LEAD) % GRP
                        nxt = 2 * n + ahead
                        a = GRP * nxt + ga
                        wait(dve, a_done, a + 1)
                        if ga == 0:
                            wait(dve, max_split, nxt - 1)
                        dve.tensor_reduce(neg_max[:, ahead % 2, ga * HPG:(ga + 1) * HPG],
                                          ps_a[:, :].rearrange("p (j k) -> p j k", j=HPG),
                                          AX, ALU.max, negate=True).then_inc(max_done, 1)
                        if ga == GRP - 1:
                            wait(dve, max_done, a + 1)
                            wait(dve, max_turned, nxt)
                            dve.tensor_copy(neg_max_bf[:, 0, :], neg_max[:, ahead % 2, :]).then_inc(max_hi, 1)
                            wait(dve, max_hi, nxt + 1)
                            dve.tensor_tensor(neg_max_bf[:, 1, :], neg_max[:, ahead % 2, :], neg_max_bf[:, 0, :],
                                              ALU.subtract).then_inc(max_split, 1)

                    if g == 3 and st.has(b - 1):
                        t = 2 * n + b - 1
                        pt, bt = st.par(b - 1), 1 - b
                        wait(dve, proj_done, t + 1)
                        wait(dve, res_ready, st.block(b - 1) + 1)
                        wait(dve, x2_ready, t - 3)
                        dve.tensor_tensor(x1[:, pt, bt, :], ps_m[:, 0:D], x_res[:, pt, bt, :],
                                          ALU.add).then_inc(x1_ready, 1)

                    if u == 3 and st.has(-1):
                        wait(dve, x1_ready, SEQ * n)
                        moments(1, x1[:, st.par(-1)], n - 1, xn2_ready)

                    if g == 1 and st.has(b - 1):
                        t = 2 * n + b - 1
                        wait(dve, o_turned, t + 1)
                        wait(dve, o_tok_ready, 2 * t)
                        o_v = ps_t[:, :].rearrange("p (r i c w) -> p r i c w", r=2, i=2, c=GRP)
                        tok_v = o_tok[:, :].rearrange("p (r c i d) -> p r c i d", r=2, c=GRP, i=2)
                        for i in range(2):
                            dve.reciprocal(o_inv[:, i], o_v[:, :, i, :, VW * i + HD]).then_inc(o_inv_done, 1)
                        wait(dve, o_inv_done, 2 * t + 2)
                        wait(dve, otok_turned, t)
                        for i in range(2):
                            dve.tensor_tensor(tok_v[:, :, :, i, :], o_v[:, :, i, :, VW * i:VW * i + HD],
                                              o_inv[:, i].unsqueeze(3).to_broadcast([S, 2, GRP, HD]),
                                              ALU.mult).then_inc(o_tok_ready, 1)
                    if u < HID_T and st.has(-2):
                        c = HID_T * (n - 2) + u
                        wait(dve, th_ready, c + 1)
                        wait(dve, h_ready, c)
                        dve.scalar_tensor_tensor(out=gated[:, :], in0=th[:, :], scalar=1.0, in1=ffn_bank[u][:, 0:T],
                                                 op0=ALU.add, op1=ALU.mult).then_inc(gated_done, 1)
                        wait(dve, gated_done, c + 1)
                        wait(dve, down_done, SEQ * (n - 2))
                        dve.tensor_tensor(hT[:, u, :], gated[:, :], ffn_bank[u][:, T:2 * T],
                                          ALU.mult).then_inc(h_ready, 1)

                    if u == 0 and st.has(2):
                        wait(dve, x_loaded[st.par(2)], DMA * (st.half(2) + 1))
                        moments(0, x_in[:, st.par(2)], n + 2, xn_ready)

                    if u in (4, 5) and st.has(-2):
                        s = u - 4
                        wait(dve, down_done, SEQ * (n - 2) + s + 1)
                        wait(dve, stored[p], DMA * st.half(-2))
                        dve.tensor_tensor(x2[:, p, s, :], ps_m[:, 0:D], x1[:, p, s, :],
                                          ALU.add).then_inc(x2_ready, 1)

                    for w, c, src, tile, at in (("k", 1, ps_g[0], k_new, (5, 5, 6, 6)),
                                                ("q", 0, ps_g[1], plain["q"][:, p], (6, 7, 7, 7))):
                        for gg in range(GRP):
                            if at[gg] == u and st.has(2):
                                wait(dve, hi_ready[w], GRP * (n + 3))
                                dve.scalar_tensor_tensor(out=tile[ROWS * LO[w]:ROWS * (LO[w] + 1), gg, :],
                                                         in0=src[ROWS * gg:ROWS * (gg + 1), 0:T],
                                                         scalar=b_grp[:, c, gg:gg + 1],
                                                         in1=tile[0:ROWS, gg, :].bitcast(F32),
                                                         op0=ALU.add, op1=ALU.subtract).then_inc(lo_ready[w], 1)

            dve.memset(one[:, :], 1.0).then_inc(consts_set, 1)
            dve.memset(ps_o[:, :], 0.0).then_inc(consts_set, 1)
            dve.memset(v_ones[:, :, :, :, :], 1.0).then_inc(consts_set, 1)
            dve.memset(neg_max_T[:, :, :], 0.0).then_inc(consts_set, 1)
            dve.wait_ge(ident_set, 2)
            dve.tensor_copy(ident_bf[:, :], ident[:, :]).then_inc(consts_set, 1)
            dve.wait_ge(consts_set, 5)
            dve.tensor_tensor(head_sel[:, :, :], ident_bf[:, 0:HEADS].unsqueeze(2).to_broadcast([D, HEADS, D]),
                              ident_bf[:, HEADS:2 * HEADS].unsqueeze(2).to_broadcast([D, HEADS, D]),
                              ALU.add).then_inc(consts_set, 1)
            dve.wait_ge(small_in, 6 * DMA)
            for w in range(2):
                dve.tensor_copy(b_row_p[:, w, :].rearrange("p (g d j) -> p g j d", g=GRP, d=HD),
                                b_row[:, w, :].rearrange("p (g j d) -> p g j d", g=GRP, d=HD)
                                ).then_inc(rows_set, 1)
            dve.tensor_copy(bv_wide[:, :], bv_col[:, 0:1].to_broadcast([D, D])).then_inc(rows_set, 1)
            dve.memset(wide["k"][:, 0].bitcast(F32), 0.0).then_inc(cleared["k"], 1)

            dve.wait_ge(attn_w_turned, 1)
            dve.wait_ge(tanh_ready, 2)
            for w, wT in enumerate((wqT, wkT)):
                dve.tensor_copy(wT[:, :].rearrange("p (g d j) -> p g j d", g=GRP, d=HD),
                                ps_g[0][:, D * w:D * (w + 1)].rearrange("p (g j d) -> p g j d", g=GRP, d=HD)
                                ).then_inc(attn_w_ready, 1)
            dve.tensor_copy(wvT[:, :], ps_g[0][:, 2 * D:3 * D]).then_inc(attn_w_ready, 1)
            dve.tensor_scalar(woT[:, :], ps_g[0][:, 3 * D:4 * D], tanh_x[:, :], None, ALU.mult).then_inc(attn_w_ready, 1)
            dve.tensor_copy(b_col[:, :], ps_m[:, 0:2]).then_inc(attn_w_ready, 1)
            dve.tensor_copy(b_grp[:, :, :], ps_m[0:ROWS, 2:2 + 2 * GRP].rearrange("p (w g) -> p w g", w=2)
                            ).then_inc(attn_w_ready, 1)
            dve.wait_ge(bias_summed, 1)
            dve.scalar_tensor_tensor(out=out_bias[:, :], in0=bo_all[:, :], scalar=tanh_x[:, :], in1=ps_a[:, 0:D],
                                     op0=ALU.mult, op1=ALU.add).then_inc(bias_ready, 1)
            step(Step(-1, 0, NB))
            dve.wait_ge(ffn_w_turned, 1)
            dve.tensor_scalar(dnT[:, :, :], ps_t[:, 0:HID_T * D].rearrange("p (t d) -> p t d", t=HID_T),
                              tanh_f[:, :], 0.5, ALU.mult, ALU.mult).then_inc(dn_w_ready, 1)
            dve.memset(wide["k"][:, 1].bitcast(F32), 0.0).then_inc(cleared["k"], 1)
            run(dve, step, -1, LAST, LOOP_FIRST, LOOP_LAST)

        @block.scalar
        def _(act):
            def step(st):
                n, p = st.n, st.p
                for u in range(8):
                    b, g = u // GRP, u % GRP
                    seq = 2 * n + b
                    slot = GRP * seq + g
                    t = seq - 1

                    if st.has(0):
                        wait(act, b_done, slot + 1)
                        wait(act, av_done, slot - 1)
                        act.activation(probs[:, u % 2, :], ps_b[u % 2][:, :], ACT.Exp,
                                       scale=SCORE_SCALE).then_inc(exp_done, 1)
                    if g == 0 and st.has(b - 1):
                        wait(act, av_done, GRP * (t + 1))
                        wait(act, o_turned, t)
                        act.copy(o_raw[:, :, :, :], ps_o[:, :].rearrange("p (r i q) -> p r i q", r=2, i=2)
                                 ).then_inc(o_raw_ready, 1)
                    if u < HID_T and st.has(-2):
                        c = HID_T * (n - 2) + u
                        wait(act, gu_done, c + 1)
                        wait(act, gated_done, c)
                        act.activation(th[:, :], ffn_bank[u][:, 0:T], ACT.Tanh, scale=0.5).then_inc(th_ready, 1)
                    if g == 2 and st.has(b - 1):
                        wait(act, otok_turned, t + 1)
                        wait(act, proj_done, t)
                        act.copy(oT[:, :], ps_t[:, 0:S]).then_inc(oT_ready, 1)
                    if g == 3 and st.has((b + 1) // SEQ):
                        wait(act, max_turned, seq + 2)
                        wait(act, b_done, GRP * seq)
                        act.copy(neg_max_T[0:2 * HEADS, 1 - b, :], ps_t_bf[0:2 * HEADS, 0:S]).then_inc(max_T_ready, 1)
                    if u == 3 and st.has(1):
                        wait(act, v_done, n + 2)
                        wait(act, av_done, 8 * n)
                        act.copy(v_ones[:, st.par(1), :, :, 0:HD],
                                 ps_g[0][:, 0:T].rearrange("p (b h d) -> p b h d", b=SEQ, h=HEADS)
                                 ).then_inc(v_ready, 1)
                    if u == 3 and st.has(2):
                        wait(act, xc_turned, n + 3)
                        wait(act, v_done, n + 2)
                        wait(act, q_done, n + 2)
                        act.copy(xcT[:, :, :], ps_g[1][:, :].rearrange("p (w t) -> p w t", w=2)).then_inc(xcT_ready, 1)
                    if u == 4 and st.has(2):
                        wait(act, k_done, n + 3)
                        wait(act, a_done, 8 * (n + 1))
                        wait(act, wide_landed["k"][st.par(1)], WD * (st.half(1) + 1))
                        wait(act, plain_landed["k"][st.par(1)], DMA * (st.half(1) + 1))
                        for gg in range(GRP):
                            rows = slice(ROWS * gg, ROWS * (gg + 1))
                            act.activation(k_new[0:ROWS, gg, :], ps_g[0][rows, 0:T], ACT.Identity,
                                           bias=b_col[rows, 1:2]).then_inc(hi_ready["k"], 1)
                    if u == 5 and st.has(2):
                        wait(act, q_done, n + 3)
                        wait(act, a_done, 8 * (n + 1))
                        for gg in range(GRP):
                            rows = slice(ROWS * gg, ROWS * (gg + 1))
                            act.activation(plain["q"][0:ROWS, p, gg, :], ps_g[1][rows, 0:T], ACT.Identity,
                                           bias=b_col[rows, 0:1]).then_inc(hi_ready["q"], 1)
                    if u == 6 and st.has(-1):
                        wait(act, xn2_turned, n)
                        wait(act, gu_done, HID_T * (n - 1))
                        act.copy(xn2T[:, :], ps_m[:, 0:T]).then_inc(xn2T_ready, 1)

            act.wait_ge(small_in, 6 * DMA)
            act.activation(tanh_x[:, :], gates[:, 0:1], ACT.Tanh).then_inc(tanh_ready, 1)
            act.activation(tanh_f[:, :], gates[:, 1:2], ACT.Tanh).then_inc(tanh_ready, 1)
            act.wait_ge(w_ffn_in, 3 * DMA)
            act.activation(gu_nat[:, :, :, :], gu_int[:, :, :, :], ACT.Copy, scale=W_SCALE).then_inc(ffn_w_f32, 1)
            act.activation(dn_nat[:, :, :], dn_int[:, :, :], ACT.Copy, scale=W_SCALE).then_inc(ffn_w_f32, 1)
            act.wait_ge(consts_set, 6)
            act.wait_ge(attn_w_ready, 6)
            step(Step(-1, 0, NB))
            act.wait_ge(ffn_w_turned, 1)
            for w in range(2):
                act.copy(guT[:, w, :, :], ps_b[w][:, 0:HID_T * D].rearrange("p (t d) -> p t d", t=HID_T)
                         ).then_inc(gu_w_ready, 1)
            run(act, step, -1, LAST, LOOP_FIRST, LOOP_LAST)

        @block.tensor
        def _(pe):
            def values(n, b, g, par):
                seq = SEQ * n + b
                wait(pe, exp_done, GRP * seq + g + 1)
                if g == 0:
                    wait(pe, o_raw_ready, seq)
                    wait(pe, v_ready, n + 1)
                for jj in range(2):
                    pair = 2 * g + jj
                    r, c = pair // GRP, pair % GRP
                    mm = pe.matmul(ps_o[32 * c:32 * c + 2 * VW, r * 2 * S:(r + 1) * 2 * S],
                                   v_ones[:, par, b, 2 * pair:2 * pair + 2, :],
                                   probs[:, g % 2, jj * 2 * S:(jj + 1) * 2 * S], start=True, stop=True)
                mm.then_inc(av_done, 1)

            def step(st):
                n, p = st.n, st.p
                for u in range(8):
                    b, g = u // GRP, u % GRP
                    seq = 2 * n + b
                    slot = GRP * seq + g
                    t = seq - 1

                    kb = (u + LEAD) // 8
                    if st.has(kb):
                        a = slot + LEAD
                        ga, nb, pp = (u + LEAD) % GRP, (u + LEAD) // GRP % 2, st.par(kb)
                        if u + LEAD == 8:
                            wait(pe, lo_ready["q"], GRP * (st.block(kb) + 1))
                            wait(pe, plain_landed["q"][pp], DMA * (st.half(kb) + 1))
                            wait(pe, wide_landed["k"][pp], WD * (st.half(kb) + 1))
                        wait(pe, max_done, a)
                        pe.matmul(ps_a[:, :], plain["q"][:, pp, ga, nb * S:(nb + 1) * S],
                                  wide["k"][:, pp, ga, :, nb * S:(nb + 1) * S],
                                  start=True, stop=True).then_inc(a_done, 1)

                    if st.has(0):
                        if u == 0:
                            wait(pe, plain_landed["k"][p], DMA * (st.half(0) + 1))
                            wait(pe, wide_landed["q"][p], WD * (st.half(0) + 1))
                        wait(pe, exp_done, slot - 1)
                        pe.matmul(ps_b[u % 2][:, :], plain["k"][:, p, g, b * S:(b + 1) * S],
                                  wide["q"][:, p, g, :, b * S:(b + 1) * S],
                                  start=True, stop=False, skip_group_check=True)
                        wait(pe, max_T_ready, seq + 1)
                        for j in range(HPG):
                            mm = pe.matmul(ps_b[u % 2][:, S * j:S * (j + 1)], head_sel[:, HPG * g + j, :],
                                           neg_max_T[:, b, :], start=False, stop=(j == HPG - 1),
                                           skip_group_check=True)
                        mm.then_inc(b_done, 1)

                    if u == 0 and st.has(-1):
                        values(n - 1, 1, GRP - 1, st.par(-1))
                    elif u > 0 and st.has(0):
                        values(n, (u - 1) // GRP, (u - 1) % GRP, p)

                    if g == 1 and st.has(b - 1):
                        wait(pe, o_raw_ready, t + 1)
                        wait(pe, max_T_ready, seq + 1)
                        for r in range(2):
                            for i in range(2):
                                mm = pe.transpose(ps_t[:, (2 * r + i) * S:(2 * r + i + 1) * S], o_raw[:, r, i, :],
                                                  ident[:, :])
                        mm.then_inc(o_turned, 1)

                    if g == 2 and st.has(b - 1):
                        wait(pe, o_tok_ready, 2 * (t + 1))
                        pe.transpose(ps_t[:, 0:S], o_tok[:, :], ident[:, :]).then_inc(otok_turned, 1)

                    if g == 3 and st.has((b + 1) // SEQ):
                        wait(pe, max_split, seq + 2)
                        wait(pe, oT_ready, t + 1)
                        wait(pe, max_T_ready, seq + 1)
                        pe.transpose(ps_t_bf[0:2 * HEADS, 0:S],
                                     neg_max_bf[:, :, :].rearrange("p w h -> p (w h)"),
                                     ident_bf[:, :]).then_inc(max_turned, 1)

                    if u < HID_T and st.has(-2):
                        c = HID_T * (n - 2) + u
                        wait(pe, xn2T_ready, n - 1)
                        if u == 0:
                            wait(pe, x1_ready, SEQ * n - 1)
                        else:
                            wait(pe, lo_ready["kq"[u - 1]], GRP * (n + 2))
                        for w in range(2):
                            mm = pe.matmul(ffn_bank[u][:, T * w:T * (w + 1)], guT[:, w, u, :], xn2T[:, :],
                                           start=True, stop=True)
                        mm.then_inc(gu_done, 1)

                    if g == 3 and st.has(b - 1):
                        wait(pe, oT_ready, t + 1)
                        wait(pe, x1_ready, t)
                        if b == 0:
                            wait(pe, h_ready, HID_T * (n - 2) + 1)
                        else:
                            wait(pe, xn2T_ready, n)
                        pe.matmul(ps_m[:, 0:D], oT[:, :], woT[:, :], start=True, stop=True).then_inc(proj_done, 1)

                    if u == 3 and st.has(1):
                        wait(pe, xcT_ready, n + 2)
                        wait(pe, lo_ready["k"], GRP * (n + 2))
                        wait(pe, h_ready, HID_T * (n - 2) + 2)
                        for s in range(SEQ):
                            mm = pe.matmul(ps_g[0][:, D * s:D * (s + 1)], xcT[:, 1, S * s:S * (s + 1)], wvT[:, :],
                                           start=True, stop=True)
                        mm.then_inc(v_done, 1)

                    if u == 3 and st.has(2):
                        wait(pe, xn_ready, n + 3)
                        wait(pe, c_loaded[st.par(2)], DMA * (st.half(2) + 1))
                        wait(pe, lo_ready["q"], GRP * (n + 2))
                        wait(pe, h_ready, HID_T * (n - 1))
                        for s in range(SEQ):
                            pe.transpose(ps_g[1][:, S * s:S * (s + 1)], xn[:, s, :], ident[:, :])
                            mm = pe.transpose(ps_g[1][:, T + S * s:T + S * (s + 1)], c_in[:, st.par(2), s, :],
                                              ident[:, :])
                        mm.then_inc(xc_turned, 1)

                    if u in (4, 5) and st.has(-2):
                        s = u - 4
                        wait(pe, h_ready, HID_T * (n - 1))
                        wait(pe, x1_ready, SEQ * n)
                        wait(pe, x2_ready, SEQ * (n - 2) + s)
                        for c in range(HID_T):
                            mm = pe.matmul(ps_m[:, 0:D], hT[:, c, S * s:S * (s + 1)], dnT[:, c, :],
                                           start=(c == 0), stop=(c == HID_T - 1))
                        mm.then_inc(down_done, 1)

                    if u == 4 and st.has(2):
                        wait(pe, xcT_ready, n + 3)
                        wait(pe, v_ready, n + 2)
                        pe.matmul(ps_g[0][:, 0:T], wkT[:, :], xcT[:, 1, :], start=True, stop=True).then_inc(k_done, 1)
                    if u == 5 and st.has(2):
                        wait(pe, xcT_ready, n + 3)
                        pe.matmul(ps_g[1][:, 0:T], wqT[:, :], xcT[:, 0, :], start=True, stop=True).then_inc(q_done, 1)

                    if u == 6 and st.has(-1):
                        wait(pe, xn2_ready, n)
                        wait(pe, x1_ready, SEQ * n)
                        wait(pe, x2_ready, SEQ * (n - 1))
                        for s in range(SEQ):
                            mm = pe.transpose(ps_m[:, S * s:S * (s + 1)], xn2[:, s, :], ident[:, :])
                        mm.then_inc(xn2_turned, 1)

            pe.wait_ge(ident_set, 2)
            pe.wait_ge(w_attn_in, 4 * DMA)
            for w in range(4):
                pe.transpose(ps_g[0][:, D * w:D * (w + 1)], w_nat[:, w, :], ident[:, :])
            pe.wait_ge(rows_set, 3)
            pe.wait_ge(consts_set, 6)
            for w in range(2):
                pe.matmul(ps_m[:, w:w + 1], b_row_p[0:1, w, :], one[0:1, 0:1], start=True, stop=True)
                for g in range(GRP):
                    at = 2 + GRP * w + g
                    mm = pe.matmul(ps_m[0:ROWS, at:at + 1], b_row_p[0:1, w, ROWS * g:ROWS * (g + 1)],
                                   one[0:1, 0:1], start=True, stop=True)
            mm.then_inc(attn_w_turned, 1)
            pe.wait_ge(attn_w_ready, 6)
            pe.matmul(ps_a[:, 0:D], bv_wide[:, :], woT[:, :], start=True, stop=True).then_inc(bias_summed, 1)
            step(Step(-1, 0, NB))
            pe.wait_ge(ffn_w_f32, 2)
            for t in range(HID_T):
                for w in range(2):
                    pe.transpose(ps_b[w][:, D * t:D * (t + 1)], gu_nat[:, w, t, :], ident[:, :])
                mm = pe.transpose(ps_t[:, D * t:D * (t + 1)], dn_nat[:, t, :], ident[:, :])
            mm.then_inc(ffn_w_turned, 1)
            pe.wait_ge(bias_ready, 1)
            pe.wait_ge(dn_w_ready, 1)
            step(Step(-1, 1, NB))
            pe.wait_ge(gu_w_ready, 2)
            run(pe, step, 0, LAST, LOOP_FIRST, LOOP_LAST)


INPUTS = ["x", "ctx_1024", "g_xattn", "g_ffn", "L0_xattn_Wq", "L0_xattn_bq", "L0_xattn_Wk", "L0_xattn_bk",
          "L0_xattn_Wv", "L0_xattn_bv", "L0_xattn_Wo", "L0_xattn_bo", "L0_ffn_w_gate", "L0_ffn_w_up",
          "L0_ffn_w_down"]


def kernel(**inputs):
    import numpy as np
    import concourse.bacc as bacc
    from concourse.bass_utils import run_bass_kernel_spmd

    nc = bacc.Bacc("TRN2", target_bir_lowering=False, num_devices=1)
    arrays, args = {}, []
    for name in INPUTS:
        a = np.ascontiguousarray(inputs[name])
        arrays[f"in_{name}"] = a
        args.append(nc.dram_tensor(f"in_{name}", a.shape, mybir.dt.from_np(a.dtype), kind="ExternalInput").ap())
    shape = arrays["in_x"].shape
    out = nc.dram_tensor("out_x", shape, F32, kind="ExternalOutput").ap()
    build(nc, *args, out)
    result = run_bass_kernel_spmd(nc, [arrays], core_ids=[0])
    return result.results[0]["out_x"]
```

```python
from contextlib import ExitStack

import concourse.bass as bass
from concourse import mybir

F32 = mybir.dt.float32
F32R = mybir.dt.float32r
BF16 = mybir.dt.bfloat16
I32 = mybir.dt.int32
ALU = mybir.AluOpType
ACT = mybir.ActivationFunctionType
AX = mybir.AxisListType.X

D = 128
S = 128
HD = 8
GRP = 4
HPG = 4
HEADS = GRP * HPG
ROWS = HPG * HD
NSLOT = 3
KROWS = NSLOT * ROWS
MROWS = KROWS + 2
SEQ = 2
T = SEQ * S
HID_T = 3
PAIRS = HEADS // 2
VW = HD + 1
EPS = 1e-5
W_SCALE = 1.0 / 127.0
LEAD = 7
SCORE_SCALE = float(HD) ** -0.5
DMA = 16
HI = 0
LO = {"q": 2, "k": 1}
COPY = {"q": 1, "k": 2}


class Step:

    def __init__(self, i, p, blocks):
        self.i, self.p, self.blocks = i, p, blocks
        self.n = 2 * i + p

    def block(self, k):
        return 2 * self.i + (self.p + k)

    def par(self, k):
        return (self.p + k) % 2

    def half(self, k):
        return self.i + (self.p + k) // 2

    def has(self, k):
        return not isinstance(self.n, int) or 0 <= self.n + k < self.blocks


def build(nc, x, ctx_in, g_xattn, g_ffn, Wq, bq, Wk, bk, Wv, bv, Wo, bo, w_gate, w_up, w_down, out):
    NB = x.shape[0] // SEQ
    x_v = x.rearrange("(n b) t c -> n t b c", b=SEQ)
    c_v = ctx_in.rearrange("(n b) t c -> n t b c", b=SEQ)
    out_v = out.rearrange("(n b) t c -> n t b c", b=SEQ)

    with ExitStack() as stack:
        def sb(name, shape, dt=F32):
            return stack.enter_context(nc.sbuf_tensor(name, shape, dt))

        totals = {}

        def sem(name, total):
            s = stack.enter_context(nc.semaphore(name))
            totals[s] = total
            return s

        def wait(eng, s, count):
            if isinstance(count, int):
                count = min(count, totals[s])
                if count <= 0:
                    return
            eng.wait_ge(s, count)

        w_nat = sb("w_nat", [D, 4, D])
        gu_int = sb("gu_int", [D, 2, HID_T, D], I32)
        dn_int = sb("dn_int", [D, HID_T, D], I32)
        gu_nat = sb("gu_nat", [D, 2, HID_T, D])
        dn_nat = sb("dn_nat", [D, HID_T, D])
        wqT, wkT, wvT, woT = (sb(n, [D, D]) for n in ("wqT", "wkT", "wvT", "woT"))
        guT = sb("guT", [D, 2, HID_T, D])
        dnT = sb("dnT", [D, HID_T, D])
        ident = sb("ident", [D, D])
        ident_bf = sb("ident_bf", [D, D], BF16)
        b_row = sb("b_row", [1, 2, D])
        b_row_p = sb("b_row_p", [1, 2, D])
        b_col = sb("b_col", [D, 2])
        b_grp = sb("b_grp", [ROWS, 2, GRP])
        one = sb("one", [1, 1])
        bv_col = sb("bv_col", [D, 1])
        bv_wide = sb("bv_wide", [D, D])
        bo_all = sb("bo_all", [D, D])
        gates = sb("gates", [D, 2])
        tanh_x = sb("tanh_x", [D, 1])
        tanh_f = sb("tanh_f", [D, 1])
        out_bias = sb("out_bias", [D, D])
        wait_word = sb("wait_word", [1, 2, SEQ])
        neg_half = sb("neg_half", [D, SEQ])

        x_in = sb("x_in", [S, 2, SEQ, D])
        c_in = sb("c_in", [S, 2, SEQ, D])
        x_res = sb("x_res", [S, 2, SEQ, D])
        stats = sb("stats", [S, 2, SEQ, 6])
        mean_var = sb("mean_var", [S, 2, SEQ, 2])
        var_eps = sb("var_eps", [S, 2, SEQ])
        rstd = sb("rstd", [S, 2, SEQ])
        xn = sb("xn", [S, SEQ, D])
        xcT = sb("xcT", [D, 2, 2, T])
        k_new = sb("k_new", [KROWS, 2, GRP, T], F32R)
        plain = {w: sb(f"{w}_plain", [r, 2, GRP, T], F32R) for w, r in (("q", KROWS), ("k", MROWS))}
        wide = {w: sb(f"{w}_wide", [r, 2, GRP, HPG, T], F32R) for w, r in (("q", MROWS), ("k", KROWS))}
        v_ones = sb("v_ones", [S, 2, SEQ, HEADS, VW])
        neg_max = sb("neg_max", [S, 2, HEADS])
        neg_max_bf = sb("neg_max_bf", [S, 2, HEADS], BF16)
        neg_max_T = sb("neg_max_T", [2 * HEADS, SEQ, S], F32R)
        probs = sb("probs", [S, 2, HPG * S])
        o_raw = sb("o_raw", [D, 2, 2, S])
        o_inv = sb("o_inv", [S, 2, 2, GRP])
        o_tok = sb("o_tok", [S, D])
        oT = sb("oT", [D, S])
        x1 = sb("x1", [S, 2, SEQ, D])
        xn2 = sb("xn2", [S, SEQ, D])
        xn2T = sb("xn2T", [D, T])
        th = sb("th", [D, HID_T, T])
        up = sb("up", [D, HID_T, T])
        gated = sb("gated", [D, HID_T, T])
        hT = sb("hT", [D, HID_T, T])
        x2 = sb("x2", [S, 2, SEQ, D])

        def bank(name):
            return stack.enter_context(nc.psum_tensor(name, [128, 512], F32))

        ps_a = bank("ps_a")
        ps_b = bank("ps_b")
        ps_o = bank("ps_o")
        ps_t = bank("ps_t")
        ps_s = bank("ps_s")
        ps_k = bank("ps_k")
        ps_q = bank("ps_q")
        ps_m = bank("ps_m")
        ffn_bank = [ps_m, ps_k, ps_m]
        ps_s_bf = ps_s[:, :].bitcast(BF16)

        BT = NB * SEQ
        w_qk_in = sem("w_qk_in", 2 * DMA)
        b_qk_in = sem("b_qk_in", 2 * DMA)
        w_vo_in = sem("w_vo_in", 2 * DMA)
        w_ffn_in = sem("w_ffn_in", 3 * DMA)
        small_in = sem("small_in", 4 * DMA)
        x_loaded = [sem(f"x_loaded{i}", NB // 2 * DMA) for i in range(2)]
        c_loaded = [sem(f"c_loaded{i}", NB // 2 * DMA) for i in range(2)]
        res_loaded = [sem(f"res_loaded{i}", NB // 2 * DMA) for i in range(2)]
        WD = HPG * DMA
        k_copied = sem("k_copied", NB * DMA)
        plain_landed = {w: [sem(f"{w}_plain_landed{i}", NB // 2 * DMA) for i in range(2)] for w in "qk"}
        wide_landed = {w: [sem(f"{w}_wide_landed{i}", NB // 2 * WD) for i in range(2)] for w in "qk"}
        max_landed = [sem(f"max_landed{b}", NB * 2 * DMA) for b in range(SEQ)]
        stored = [sem(f"stored{i}", NB // 2 * DMA) for i in range(2)]
        ident_set = sem("ident_set", 3)
        cleared = {"k": sem("k_cleared", 2), "q": sem("q_cleared", 2)}
        rows_set = sem("rows_set", 2)
        ones_set = sem("ones_set", 1)
        bv_set = sem("bv_set", 1)
        consts_set = sem("consts_set", 4)
        ffn_w_f32 = sem("ffn_w_f32", 2)
        tanh_ready = sem("tanh_ready", 2)
        qk_w_turned = sem("qk_w_turned", 1)
        qk_w_ready = sem("qk_w_ready", 4)
        vo_w_turned = sem("vo_w_turned", 1)
        vo_w_ready = sem("vo_w_ready", 2)
        bias_summed = sem("bias_summed", 1)
        bias_ready = sem("bias_ready", 1)
        ffn_w_turned = sem("ffn_w_turned", 1)
        gu_w_ready = sem("gu_w_ready", 2)
        dn_w_ready = sem("dn_w_ready", 1)
        a_done = sem("a_done", BT * GRP)
        b_done = sem("b_done", BT * GRP)
        av_done = sem("av_done", BT * GRP)
        max_turned = sem("max_turned", BT)
        o_turned = sem("o_turned", BT)
        otok_turned = sem("otok_turned", BT)
        proj_done = sem("proj_done", BT)
        gu_done = sem("gu_done", NB * HID_T)
        down_done = sem("down_done", BT)
        v_done = sem("v_done", NB)
        xc_turned = sem("xc_turned", NB)
        k_done = sem("k_done", NB)
        q_done = sem("q_done", NB)
        xn2_turned = sem("xn2_turned", NB)
        max_T_ready = sem("max_T_ready", BT)
        exp_done = sem("exp_done", BT * GRP)
        o_raw_ready = sem("o_raw_ready", BT)
        oT_ready = sem("oT_ready", BT)
        v_ready = sem("v_ready", NB)
        xcT_ready = sem("xcT_ready", NB)
        hi_ready = {w: sem(f"{w}_hi_ready", NB * GRP) for w in "qk"}
        xn2T_ready = sem("xn2T_ready", NB)
        th_ready = sem("th_ready", NB * HID_T)
        up_ready = sem("up_ready", NB * HID_T)
        max_done = sem("max_done", BT * GRP)
        max_hi = sem("max_hi", BT)
        max_split = sem("max_split", BT)
        lo_ready = {w: sem(f"{w}_lo_ready", NB * GRP) for w in "qk"}
        stats_done = [sem("stats1_done", BT), sem("stats2_done", BT)]
        mean_var_done = [sem("mean_var1_done", BT), sem("mean_var2_done", BT)]
        var_ready = [sem("var1_ready", NB), sem("var2_ready", NB)]
        gated_done = sem("gated_done", NB * HID_T)
        o_inv_done = sem("o_inv_done", BT)
        o_tok_ready = sem("o_tok_ready", 2 * BT)
        x1_ready = sem("x1_ready", BT)
        x2_ready = sem("x2_ready", NB)
        rstd_done = [sem("rstd1_done", NB), sem("rstd2_done", NB)]
        centred = [sem("centred1", NB), sem("centred2", NB)]
        xn_ready = sem("xn_ready", NB)
        xn2_ready = sem("xn2_ready", NB)
        res_ready = sem("res_ready", NB)
        h_ready = sem("h_ready", NB * HID_T)

        def run(eng, step, first, last, loop_first, loop_last):
            for n in range(first, loop_first):
                step(Step(n // 2, n % 2, NB))
            with eng.Fori(loop_first // 2, (loop_last + 1) // 2) as i:
                for p in range(2):
                    step(Step(i, p, NB))
            for n in range(loop_last + 1, last + 1):
                step(Step(n // 2, n % 2, NB))

        LAST = NB + 2
        LOOP_FIRST, LOOP_LAST = 6, NB - 5

        block = stack.enter_context(nc.Block())

        @block.sync
        def _(sp):
            def load_inputs(st, k):
                if st.has(k):
                    n, p = st.block(k), st.par(k)
                    wait(sp, xn_ready, n - 1)
                    sp.dma_start(x_in[:, p], x_v[n]).then_inc(x_loaded[p], DMA)
                    wait(sp, xc_turned, n - 1)
                    sp.dma_start(c_in[:, p], c_v[n]).then_inc(c_loaded[p], DMA)

            def load_residual(st):
                if st.has(0):
                    wait(sp, x1_ready, SEQ * (st.n - 1))
                    sp.dma_start(x_res[:, st.p], x_v[st.block(0)]).then_inc(res_loaded[st.p], DMA)

            def store(st):
                if st.has(-3):
                    wait(sp, x2_ready, st.n - 2)
                    sp.dma_start(out_v[st.block(-3)], x2[:, st.par(-3)]).then_inc(stored[st.par(-3)], DMA)

            def place_maxima(st, b):
                k = 1 - b
                if st.has(k):
                    wait(sp, max_T_ready, 2 * st.n + 3 - b)
                    for part in range(2):
                        sp.dma_start(wide["q"][KROWS + part:KROWS + part + 1, st.par(k), :, :, b * S:(b + 1) * S
                                               ].bitcast(F32),
                                     neg_max_T[HEADS * part:HEADS * (part + 1), b, :].bitcast(F32)
                                     ).then_inc(max_landed[b], DMA)

            def copy_high(st, w):
                if st.has(2):
                    tile, landed = ((k_new[:, st.p], k_copied) if w == "k" else
                                    (plain["q"][:, st.p], plain_landed["q"][st.p]))
                    wait(sp, hi_ready[w], GRP * (st.n + 3))
                    sp.dma_start(tile[ROWS * COPY[w]:ROWS * (COPY[w] + 1)].bitcast(F32),
                                 tile[0:ROWS].bitcast(F32)).then_inc(landed, DMA)

            def widen(st, w):
                if st.has(2):
                    n, p = st.n, st.p
                    src = k_new[:, p] if w == "k" else plain["q"][:, p]
                    if isinstance(n, int) and n < 0:
                        wait(sp, cleared[w], n + 3)
                    wait(sp, lo_ready[w], GRP * (n + 3))
                    for j in range(HPG):
                        sp.dma_start(wide[w][j:KROWS:HPG, p, :, j, :].bitcast(F32),
                                     src[j:KROWS:HPG].bitcast(F32)).then_inc(wide_landed[w][p], DMA)

            def copy_k(st):
                if st.has(2):
                    wait(sp, b_done, 8 * (st.n + 1))
                    sp.dma_start(plain["k"][0:KROWS, st.p].bitcast(F32), k_new[:, st.p].bitcast(F32)
                                 ).then_inc(plain_landed["k"][st.p], DMA)

            def step(st):
                place_maxima(st, 1)
                copy_high(st, "k")
                store(st)
                load_residual(st)
                copy_high(st, "q")
                widen(st, "k")
                place_maxima(st, 0)
                load_inputs(st, 4)
                copy_k(st)
                widen(st, "q")

            load_inputs(Step(0, 0, NB), 0)
            sp.dma_start(w_nat[:, 1, :], Wk).then_inc(w_qk_in, DMA)
            sp.dma_start(b_row[:, 1, :], bk.unsqueeze(0)).then_inc(b_qk_in, DMA)
            sp.dma_start(w_nat[:, 0, :], Wq).then_inc(w_qk_in, DMA)
            sp.dma_start(b_row[:, 0, :], bq.unsqueeze(0)).then_inc(b_qk_in, DMA)
            load_inputs(Step(0, 1, NB), 0)
            sp.dma_start(w_nat[:, 2, :], Wv).then_inc(w_vo_in, DMA)
            sp.dma_start(w_nat[:, 3, :], Wo).then_inc(w_vo_in, DMA)
            sp.dma_start(gates[:, 0:1], g_xattn.partition_broadcast(D)).then_inc(small_in, DMA)
            sp.dma_start(gates[:, 1:2], g_ffn.partition_broadcast(D)).then_inc(small_in, DMA)
            sp.dma_start(bv_col[:, :], bv.unsqueeze(1)).then_inc(small_in, DMA)
            sp.dma_start(bo_all[:, :], bo.partition_broadcast(D)).then_inc(small_in, DMA)
            sp.dma_start(gu_int[:, 0], w_gate.rearrange("(t p) d -> p t d", p=D)).then_inc(w_ffn_in, DMA)
            sp.dma_start(gu_int[:, 1], w_up.rearrange("(t p) d -> p t d", p=D)).then_inc(w_ffn_in, DMA)
            sp.dma_start(dn_int[:, :, :], w_down.rearrange("p (t d) -> p t d", t=HID_T)).then_inc(w_ffn_in, DMA)
            run(sp, step, -2, LAST, LOOP_FIRST, LOOP_LAST)
            for p in range(2):
                sp.wait_ge(stored[p], NB // 2 * DMA)

        @block.gpsimd
        def _(pool):
            def normalise(which, src, dst, ready, n):
                wait(pool, var_ready[which], n + 1)
                pool.tensor_tensor(rstd[:, which, :], var_eps[:, which, :], neg_half[:, :],
                                   ALU.pow).then_inc(rstd_done[which], 1)
                wait(pool, rstd_done[which], n + 1)
                pool.tensor_tensor(dst[:, :, :], src,
                                   mean_var[:, which, :, 0].unsqueeze(2).to_broadcast([S, SEQ, D]),
                                   ALU.subtract).then_inc(centred[which], 1)
                wait(pool, centred[which], n + 1)
                pool.tensor_tensor(dst[:, :, :], dst[:, :, :],
                                   rstd[:, which, :].unsqueeze(2).to_broadcast([S, SEQ, D]),
                                   ALU.mult).then_inc(ready, 1)

            def normalise_inputs(st):
                if st.has(3):
                    wait(pool, xc_turned, st.n + 3)
                    normalise(0, x_in[:, st.par(3)], xn, xn_ready, st.block(3))

            def normalise_x1(st):
                if st.has(-2):
                    wait(pool, xn2_turned, st.n - 2)
                    normalise(1, x1[:, st.par(-2)], xn2, xn2_ready, st.block(-2))

            def add_bias(st):
                if st.has(0):
                    wait(pool, res_loaded[st.p], DMA * (st.half(0) + 1))
                    pool.tensor_tensor(x_res[:, st.p], x_res[:, st.p],
                                       out_bias[:, :].unsqueeze(1).to_broadcast([S, SEQ, D]),
                                       ALU.add).then_inc(res_ready, 1)

            def hidden(st, third):
                if st.has(-2):
                    wait(pool, gated_done, HID_T * (st.n - 2) + third + 1)
                    wait(pool, down_done, SEQ * (st.n - 2))
                    pool.tensor_tensor(hT[:, third, :], gated[:, third, :], up[:, third, :],
                                       ALU.mult).then_inc(h_ready, 1)

            def step(st):
                normalise_x1(st)
                normalise_inputs(st)
                hidden(st, 1)
                hidden(st, 0)
                add_bias(st)
                hidden(st, 2)

            pool.memset(ident[:, :], 0.0).then_inc(ident_set, 1)
            pool.wait_ge(ident_set, 1)
            pool.affine_select(out=ident[:, :], in_=ident[:, :], compare_op=ALU.not_equal, fill=1.0, base=0,
                               pattern=[[-1, D]], channel_multiplier=1).then_inc(ident_set, 1)
            pool.memset(neg_half[:, :], -0.5).then_inc(ident_set, 1)
            pool.wait_ge(ident_set, 3)
            pool.memset(wide["k"][:, 0].bitcast(F32), 0.0).then_inc(cleared["k"], 1)
            step(Step(-2, 1, NB))
            step(Step(-1, 0, NB))
            pool.memset(wide["q"][0:KROWS, 0].bitcast(F32), 0.0).then_inc(cleared["q"], 1)
            pool.memset(wide["k"][:, 1].bitcast(F32), 0.0).then_inc(cleared["k"], 1)
            pool.memset(wide["q"][0:KROWS, 1].bitcast(F32), 0.0).then_inc(cleared["q"], 1)
            step(Step(-1, 1, NB))
            pool.wait_ge(bias_ready, 1)
            run(pool, step, 0, LAST, LOOP_FIRST, LOOP_LAST)

        @block.vector
        def _(dve):
            def row_stats(which, src, m, used, b):
                if b == 0:
                    wait(dve, used, m)
                dve.bn_stats(stats[:, which, b, :], src[:, b, :]).then_inc(stats_done[which], 1)

            def mean_and_var(which, m, b):
                wait(dve, stats_done[which], SEQ * m + b + 1)
                dve.memset(wait_word[:, which, b:b + 1], 0.0)
                dve.bn_aggr(mean_var[:, which, b, :], stats[:, which, b, :]).then_inc(mean_var_done[which], 1)

            def add_eps(which, m):
                wait(dve, mean_var_done[which], SEQ * (m + 1))
                dve.tensor_scalar(var_eps[:, which, :], mean_var[:, which, :, 1], EPS, None,
                                  ALU.add).then_inc(var_ready[which], 1)

            def row_maxima(st, u):
                if st.has((u + LEAD) // 8):
                    ahead, ga = (u + LEAD) // GRP, (u + LEAD) % GRP
                    nxt = 2 * st.n + ahead
                    a = GRP * nxt + ga
                    wait(dve, a_done, a + 1)
                    if ga == 0:
                        wait(dve, max_split, nxt - 1)
                    dve.tensor_reduce(neg_max[:, ahead % 2, ga * HPG:(ga + 1) * HPG],
                                      ps_a[:, :].rearrange("p (j k) -> p j k", j=HPG),
                                      AX, ALU.max, negate=True).then_inc(max_done, 1)

            def split_high(st, b):
                if st.has((b + 1) // SEQ):
                    nxt = 2 * st.n + b + 1
                    wait(dve, max_done, GRP * (nxt + 1))
                    wait(dve, max_turned, nxt)
                    dve.tensor_copy(neg_max_bf[:, 0, :], neg_max[:, 1 - b, :]).then_inc(max_hi, 1)

            def split_low(st, b):
                if st.has((b + 1) // SEQ):
                    nxt = 2 * st.n + b + 1
                    wait(dve, max_hi, nxt + 1)
                    dve.tensor_tensor(neg_max_bf[:, 1, :], neg_max[:, 1 - b, :], neg_max_bf[:, 0, :],
                                      ALU.subtract).then_inc(max_split, 1)

            def first_residual(st, b):
                if st.has(-1):
                    wait(dve, proj_done, 2 * st.n + b - 1)
                    wait(dve, res_ready, st.n)
                    wait(dve, x2_ready, st.n - 2)
                    dve.tensor_tensor(x1[:, st.par(-1), b, :], ps_s[:, 0:D], x_res[:, st.par(-1), b, :],
                                      ALU.add).then_inc(x1_ready, 1)

            def second_residual(st):
                if st.has(-3):
                    wait(dve, down_done, SEQ * (st.n - 2))
                    wait(dve, stored[st.par(-3)], DMA * st.half(-3))
                    dve.tensor_tensor(x2[:, st.par(-3)], ps_m[:, 0:T].rearrange("p (s d) -> p s d", s=SEQ),
                                      x1[:, st.par(-3)], ALU.add).then_inc(x2_ready, 1)

            def invert(st, b):
                if st.has(b - 1):
                    t = 2 * st.n + b - 1
                    wait(dve, o_turned, t + 1)
                    wait(dve, o_tok_ready, 2 * t)
                    den = bass.AP(ps_t[:, :].tensor, HD, [ps_t[:, :].ap[0], [2 * S, 2], [S + VW, 2], [32, GRP]])
                    dve.reciprocal(o_inv[:, :, :, :], den).then_inc(o_inv_done, 1)

            def normalise(st, b):
                if st.has(b - 1):
                    t = 2 * st.n + b - 1
                    o_v = ps_t[:, :].rearrange("p (r i c w) -> p r i c w", r=2, i=2, c=GRP)
                    tok_v = o_tok[:, :].rearrange("p (r c i d) -> p r c i d", r=2, c=GRP, i=2)
                    wait(dve, o_inv_done, t + 1)
                    wait(dve, otok_turned, t)
                    for i in range(2):
                        dve.tensor_tensor(tok_v[:, :, :, i, :], o_v[:, :, i, :, VW * i:VW * i + HD],
                                          o_inv[:, :, i, :].unsqueeze(3).to_broadcast([S, 2, GRP, HD]),
                                          ALU.mult).then_inc(o_tok_ready, 1)

            def gate(st, third):
                if st.has(-2):
                    c = HID_T * (st.n - 2) + third
                    wait(dve, th_ready, c + 1)
                    wait(dve, h_ready, c - 2)
                    dve.scalar_tensor_tensor(out=gated[:, third, :], in0=th[:, third, :], scalar=1.0,
                                             in1=ffn_bank[third][:, 0:T], op0=ALU.add,
                                             op1=ALU.mult).then_inc(gated_done, 1)

            def low_part(st, w, gg):
                if st.has(2):
                    n, p = st.n, st.p
                    c, src, tile = {"k": (1, ps_k, k_new[:, p]), "q": (0, ps_q, plain["q"][:, p])}[w]
                    wait(dve, hi_ready[w], GRP * (n + 3))
                    if gg == GRP - 1:
                        if w == "k":
                            wait(dve, k_copied, DMA * (n + 3))
                        else:
                            wait(dve, plain_landed["q"][p], DMA * (st.half(2) + 1))
                    dve.scalar_tensor_tensor(out=tile[ROWS * LO[w]:ROWS * (LO[w] + 1), gg, :],
                                             in0=src[ROWS * gg:ROWS * (gg + 1), 0:T],
                                             scalar=b_grp[:, c, gg:gg + 1],
                                             in1=tile[0:ROWS, gg, :].bitcast(F32),
                                             op0=ALU.add, op1=ALU.subtract).then_inc(lo_ready[w], 1)

            def step(st):
                n = st.n
                x_new, x1_last = x_in[:, st.par(3)], x1[:, st.par(-1)]
                row_maxima(st, 0)
                if st.has(3):
                    wait(dve, x_loaded[st.par(3)], DMA * (st.half(3) + 1))
                    row_stats(0, x_new, n + 3, xn_ready, 0)
                split_high(st, 0)
                split_low(st, 0)
                row_maxima(st, 1)
                if st.has(3):
                    row_stats(0, x_new, n + 3, xn_ready, 1)
                second_residual(st)
                if st.has(3):
                    mean_and_var(0, n + 3, 0)
                    mean_and_var(0, n + 3, 1)
                    add_eps(0, n + 3)
                row_maxima(st, 2)
                invert(st, 0)
                low_part(st, "k", 0)
                normalise(st, 0)
                low_part(st, "k", 1)
                first_residual(st, 0)
                row_maxima(st, 3)
                low_part(st, "k", 2)
                low_part(st, "k", 3)
                row_maxima(st, 4)
                gate(st, 0)
                split_high(st, 1)
                low_part(st, "q", 1)
                low_part(st, "q", 0)
                split_low(st, 1)
                row_maxima(st, 5)
                low_part(st, "q", 2)
                gate(st, 1)
                row_maxima(st, 6)
                invert(st, 1)
                low_part(st, "q", 3)
                normalise(st, 1)
                first_residual(st, 1)
                gate(st, 2)
                row_maxima(st, 7)
                if st.has(-1):
                    row_stats(1, x1_last, n - 1, xn2_ready, 0)
                    wait(dve, x1_ready, SEQ * n)
                    row_stats(1, x1_last, n - 1, xn2_ready, 1)
                    mean_and_var(1, n - 1, 0)
                    mean_and_var(1, n - 1, 1)
                    add_eps(1, n - 1)

            dve.memset(one[:, :], 1.0).then_inc(consts_set, 1)
            dve.memset(ps_o[:, :], 0.0).then_inc(consts_set, 1)
            dve.memset(v_ones[:, :, :, :, :], 1.0).then_inc(consts_set, 1)
            dve.wait_ge(ident_set, 2)
            dve.tensor_copy(ident_bf[:, :], ident[:, :]).then_inc(consts_set, 1)
            step(Step(-2, 1, NB))

            dve.wait_ge(b_qk_in, 2 * DMA)
            for w in range(2):
                dve.tensor_copy(b_row_p[:, w, :].rearrange("p (g d j) -> p g j d", g=GRP, d=HD),
                                b_row[:, w, :].rearrange("p (g j d) -> p g j d", g=GRP, d=HD)
                                ).then_inc(rows_set, 1)
            dve.wait_ge(qk_w_turned, 1)
            for w, wT in enumerate((wqT, wkT)):
                dve.tensor_copy(wT[:, :].rearrange("p (g d j) -> p g j d", g=GRP, d=HD),
                                ps_q[:, D * w:D * (w + 1)].rearrange("p (g j d) -> p g j d", g=GRP, d=HD)
                                ).then_inc(qk_w_ready, 1)
            dve.tensor_copy(b_col[:, :], ps_m[:, 0:2]).then_inc(qk_w_ready, 1)
            dve.tensor_copy(b_grp[:, :, :], ps_m[0:ROWS, 2:2 + 2 * GRP].rearrange("p (w g) -> p w g", w=2)
                            ).then_inc(qk_w_ready, 1)
            step(Step(-1, 0, NB))

            dve.memset(plain["k"][KROWS:MROWS].bitcast(F32), 1.0).then_inc(ones_set, 1)
            dve.wait_ge(small_in, 4 * DMA)
            dve.tensor_copy(bv_wide[:, :], bv_col[:, 0:1].to_broadcast([D, D])).then_inc(bv_set, 1)
            dve.wait_ge(vo_w_turned, 1)
            dve.wait_ge(tanh_ready, 2)
            dve.tensor_copy(wvT[:, :], ps_t[:, 0:D]).then_inc(vo_w_ready, 1)
            dve.tensor_scalar(woT[:, :], ps_t[:, D:2 * D], tanh_x[:, :], None, ALU.mult).then_inc(vo_w_ready, 1)
            dve.wait_ge(bias_summed, 1)
            dve.scalar_tensor_tensor(out=out_bias[:, :], in0=bo_all[:, :], scalar=tanh_x[:, :], in1=ps_a[:, 0:D],
                                     op0=ALU.mult, op1=ALU.add).then_inc(bias_ready, 1)
            step(Step(-1, 1, NB))
            dve.wait_ge(ffn_w_turned, 1)
            dve.tensor_scalar(dnT[:, :, :], ps_o[:, 0:HID_T * D].rearrange("p (t d) -> p t d", t=HID_T),
                              tanh_f[:, :], 0.5, ALU.mult, ALU.mult).then_inc(dn_w_ready, 1)
            run(dve, step, 0, LAST, LOOP_FIRST, LOOP_LAST)

        @block.scalar
        def _(act):
            def exponentials(st, u):
                if st.has(0):
                    slot = 8 * st.n + u
                    wait(act, b_done, slot + 1)
                    wait(act, av_done, slot - 1)
                    act.activation(probs[:, u % 2, :], ps_b[:, :], ACT.Exp, scale=SCORE_SCALE).then_inc(exp_done, 1)

            def copy_maxima(st, b):
                k = (b + 1) // SEQ
                if st.has(k):
                    wait(act, max_turned, 2 * st.n + b + 2)
                    wait(act, max_landed[1 - b], 2 * DMA * st.block(k))
                    act.copy(neg_max_T[:, 1 - b, :], ps_s_bf[0:2 * HEADS, 0:S]).then_inc(max_T_ready, 1)

            def copy_values(st, b):
                if st.has(b - 1):
                    t = 2 * st.n + b - 1
                    wait(act, av_done, GRP * (t + 1))
                    wait(act, o_turned, t)
                    act.copy(o_raw[:, :, :, :], ps_o[:, :].rearrange("p (r i q) -> p r i q", r=2, i=2)
                             ).then_inc(o_raw_ready, 1)

            def copy_output(st, b):
                if st.has(b - 1):
                    t = 2 * st.n + b - 1
                    wait(act, otok_turned, t + 1)
                    wait(act, proj_done, t)
                    act.copy(oT[:, :], ps_t[:, 0:S]).then_inc(oT_ready, 1)

            def copy_v(st):
                if st.has(1):
                    wait(act, v_done, st.n + 2)
                    wait(act, av_done, 8 * st.n)
                    act.copy(v_ones[:, st.par(1), :, :, 0:HD],
                             ps_t[:, 0:T].rearrange("p (b h d) -> p b h d", b=SEQ, h=HEADS)).then_inc(v_ready, 1)

            def high_part(st, w, groups):
                if st.has(2):
                    n, p = st.n, st.p
                    if w == "k":
                        src, tile, bias = ps_k, k_new[:, p], 1
                        wait(act, k_done, n + 3)
                        wait(act, wide_landed["k"][p], WD * st.half(2))
                        wait(act, plain_landed["k"][p], DMA * st.half(2))
                    else:
                        src, tile, bias = ps_q, plain["q"][:, p], 0
                        wait(act, q_done, n + 3)
                        wait(act, a_done, 8 * (n + 1))
                    for gg in groups:
                        rows = slice(ROWS * gg, ROWS * (gg + 1))
                        act.activation(tile[0:ROWS, gg, :], src[rows, 0:T], ACT.Identity,
                                       bias=b_col[rows, bias:bias + 1]).then_inc(hi_ready[w], 1)

            def copy_inputs(st):
                if st.has(3):
                    wait(act, xc_turned, st.n + 4)
                    wait(act, v_done, st.n + 2)
                    wait(act, q_done, st.n + 2)
                    act.copy(xcT[:, st.par(3)], ps_k[:, :].rearrange("p (w t) -> p w t", w=2)).then_inc(xcT_ready, 1)

            def copy_xn2(st):
                if st.has(-2):
                    wait(act, xn2_turned, st.n - 1)
                    wait(act, gu_done, HID_T * (st.n - 2))
                    act.copy(xn2T[:, :], ps_m[:, 0:T]).then_inc(xn2T_ready, 1)

            def up_and_tanh(st, third):
                if st.has(-2):
                    c = HID_T * (st.n - 2) + third
                    wait(act, gu_done, c + 1)
                    wait(act, h_ready, c - 2)
                    act.copy(up[:, third, :], ffn_bank[third][:, T:2 * T]).then_inc(up_ready, 1)
                    act.activation(th[:, third, :], ffn_bank[third][:, 0:T], ACT.Tanh, scale=0.5).then_inc(th_ready, 1)

            def step(st):
                exponentials(st, 0)
                copy_values(st, 0)
                high_part(st, "k", (0, 1))
                copy_maxima(st, 0)
                exponentials(st, 1)
                high_part(st, "k", (2, 3))
                exponentials(st, 2)
                high_part(st, "q", (0, 1))
                copy_xn2(st)
                exponentials(st, 3)
                copy_output(st, 0)
                high_part(st, "q", (2, 3))
                up_and_tanh(st, 0)
                copy_v(st)
                exponentials(st, 4)
                copy_values(st, 1)
                up_and_tanh(st, 1)
                exponentials(st, 5)
                copy_maxima(st, 1)
                up_and_tanh(st, 2)
                exponentials(st, 6)
                copy_inputs(st)
                exponentials(st, 7)
                copy_output(st, 1)

            step(Step(-2, 1, NB))
            act.wait_ge(consts_set, 4)
            act.wait_ge(qk_w_ready, 4)
            step(Step(-1, 0, NB))
            act.wait_ge(small_in, 4 * DMA)
            act.activation(tanh_x[:, :], gates[:, 0:1], ACT.Tanh).then_inc(tanh_ready, 1)
            act.activation(tanh_f[:, :], gates[:, 1:2], ACT.Tanh).then_inc(tanh_ready, 1)
            act.wait_ge(w_ffn_in, 3 * DMA)
            act.activation(gu_nat[:, :, :, :], gu_int[:, :, :, :], ACT.Copy, scale=W_SCALE).then_inc(ffn_w_f32, 1)
            act.activation(dn_nat[:, :, :], dn_int[:, :, :], ACT.Copy, scale=W_SCALE).then_inc(ffn_w_f32, 1)
            step(Step(-1, 1, NB))
            act.wait_ge(ffn_w_turned, 1)
            for w in range(2):
                act.copy(guT[:, w, :, :], (ps_b, ps_m)[w][:, 0:HID_T * D].rearrange("p (t d) -> p t d", t=HID_T)
                         ).then_inc(gu_w_ready, 1)
            run(act, step, 0, LAST, LOOP_FIRST, LOOP_LAST)

        @block.tensor
        def _(pe):
            def maxima_scores(st, u):
                kb = (u + LEAD) // 8
                if st.has(kb):
                    ga, nb, pp = (u + LEAD) % GRP, (u + LEAD) // GRP % 2, st.par(kb)
                    if u + LEAD == 8:
                        wait(pe, lo_ready["q"], GRP * (st.block(kb) + 1))
                        wait(pe, plain_landed["q"][pp], DMA * (st.half(kb) + 1))
                        wait(pe, wide_landed["k"][pp], WD * (st.half(kb) + 1))
                    wait(pe, max_done, 8 * st.n + u + LEAD)
                    pe.matmul(ps_a[:, :], plain["q"][:, pp, ga, nb * S:(nb + 1) * S],
                              wide["k"][:, pp, ga, :, nb * S:(nb + 1) * S],
                              start=True, stop=True).then_inc(a_done, 1)

            def scores(st, u):
                if st.has(0):
                    n, p, b, g = st.n, st.p, u // GRP, u % GRP
                    if u == 0:
                        wait(pe, plain_landed["k"][p], DMA * (st.half(0) + 1))
                        wait(pe, wide_landed["q"][p], WD * (st.half(0) + 1))
                    if g == 0:
                        wait(pe, max_landed[b], 2 * DMA * (n + 1))
                    wait(pe, exp_done, 8 * n + u)
                    pe.matmul(ps_b[:, :], plain["k"][:, p, g, b * S:(b + 1) * S],
                              wide["q"][:, p, g, :, b * S:(b + 1) * S],
                              start=True, stop=True).then_inc(b_done, 1)

            def values(st, u):
                k, b, g = (u - 1) // 8, (u - 1) // GRP % 2, (u - 1) % GRP
                if st.has(k):
                    wait(pe, exp_done, 8 * st.n + u)
                    if g == 0:
                        wait(pe, o_raw_ready, 2 * st.n + b)
                        wait(pe, v_ready, st.n + 1)
                    for jj in range(2):
                        pair = 2 * g + jj
                        r, c = pair // GRP, pair % GRP
                        mm = pe.matmul(ps_o[32 * c:32 * c + 2 * VW, r * 2 * S:(r + 1) * 2 * S],
                                       v_ones[:, st.par(k), b, 2 * pair:2 * pair + 2, :],
                                       probs[:, g % 2, jj * 2 * S:(jj + 1) * 2 * S], start=True, stop=True)
                    mm.then_inc(av_done, 1)

            def turn_maxima(st, b):
                if st.has((b + 1) // SEQ):
                    seq = 2 * st.n + b
                    wait(pe, max_split, seq + 2)
                    wait(pe, x1_ready, seq - 2)
                    wait(pe, max_T_ready, seq + 1)
                    pe.transpose(ps_s_bf[0:2 * HEADS, 0:S], neg_max_bf[:, :, :].rearrange("p w h -> p (w h)"),
                                 ident_bf[:, :]).then_inc(max_turned, 1)

            def turn_inputs(st):
                if st.has(3):
                    n = st.n
                    wait(pe, xn_ready, n + 4)
                    wait(pe, c_loaded[st.par(3)], DMA * (st.half(3) + 1))
                    wait(pe, lo_ready["k"], GRP * (n + 3))
                    wait(pe, gated_done, HID_T * (n - 2) + 2)
                    for s in range(SEQ):
                        pe.transpose(ps_k[:, S * s:S * (s + 1)], xn[:, s, :], ident[:, :])
                        mm = pe.transpose(ps_k[:, T + S * s:T + S * (s + 1)], c_in[:, st.par(3), s, :], ident[:, :])
                    mm.then_inc(xc_turned, 1)

            def project_k(st):
                if st.has(2):
                    wait(pe, xcT_ready, st.n + 3)
                    pe.matmul(ps_k[:, 0:T], wkT[:, :], xcT[:, st.p, 1, :], start=True, stop=True).then_inc(k_done, 1)

            def project_q(st):
                if st.has(2):
                    wait(pe, xcT_ready, st.n + 3)
                    wait(pe, lo_ready["q"], GRP * (st.n + 2))
                    pe.matmul(ps_q[:, 0:T], wqT[:, :], xcT[:, st.p, 0, :], start=True, stop=True).then_inc(q_done, 1)

            def project_v(st):
                if st.has(1):
                    wait(pe, xcT_ready, st.n + 2)
                    wait(pe, oT_ready, SEQ * st.n)
                    for s in range(SEQ):
                        mm = pe.matmul(ps_t[:, D * s:D * (s + 1)], xcT[:, st.par(1), 1, S * s:S * (s + 1)],
                                       wvT[:, :], start=True, stop=True)
                    mm.then_inc(v_done, 1)

            def turn_values(st, b):
                if st.has(b - 1):
                    t = 2 * st.n + b - 1
                    wait(pe, o_raw_ready, t + 1)
                    wait(pe, oT_ready, t)
                    if b == 1:
                        wait(pe, v_ready, st.n + 2)
                    for r in range(2):
                        for i in range(2):
                            mm = pe.transpose(ps_t[:, (2 * r + i) * S:(2 * r + i + 1) * S], o_raw[:, r, i, :],
                                              ident[:, :])
                    mm.then_inc(o_turned, 1)

            def turn_output(st, b):
                if st.has(b - 1):
                    t = 2 * st.n + b - 1
                    wait(pe, o_tok_ready, 2 * (t + 1))
                    pe.transpose(ps_t[:, 0:S], o_tok[:, :], ident[:, :]).then_inc(otok_turned, 1)

            def project_output(st, b):
                if st.has(-1):
                    seq = 2 * st.n + b
                    wait(pe, oT_ready, seq - 1)
                    wait(pe, x1_ready, seq - 2)
                    wait(pe, max_T_ready, seq + 2)
                    pe.matmul(ps_s[:, 0:D], oT[:, :], woT[:, :], start=True, stop=True).then_inc(proj_done, 1)

            def turn_xn2(st):
                if st.has(-2):
                    wait(pe, xn2_ready, st.n - 1)
                    wait(pe, x2_ready, st.n - 2)
                    for s in range(SEQ):
                        mm = pe.transpose(ps_m[:, S * s:S * (s + 1)], xn2[:, s, :], ident[:, :])
                    mm.then_inc(xn2_turned, 1)

            def gate_and_up(st, third):
                if st.has(-2):
                    c = HID_T * (st.n - 2) + third
                    wait(pe, xn2T_ready, st.n - 1)
                    if third == 1:
                        wait(pe, lo_ready["k"], GRP * (st.n + 3))
                    elif third == 2:
                        wait(pe, gated_done, c - 1)
                    for w in range(2):
                        mm = pe.matmul(ffn_bank[third][:, T * w:T * (w + 1)], guT[:, w, third, :], xn2T[:, :],
                                       start=True, stop=True)
                    mm.then_inc(gu_done, 1)

            def down(st, s):
                if st.has(-3):
                    wait(pe, h_ready, HID_T * (st.n - 2))
                    for c in range(HID_T):
                        mm = pe.matmul(ps_m[:, D * s:D * (s + 1)], hT[:, c, S * s:S * (s + 1)], dnT[:, c, :],
                                       start=(c == 0), stop=(c == HID_T - 1))
                    mm.then_inc(down_done, 1)

            def step(st):
                maxima_scores(st, 0)
                down(st, 0)
                scores(st, 0)
                project_k(st)
                values(st, 0)
                maxima_scores(st, 1)
                down(st, 1)
                turn_maxima(st, 0)
                scores(st, 1)
                values(st, 1)
                maxima_scores(st, 2)
                turn_values(st, 0)
                scores(st, 2)
                project_q(st)
                values(st, 2)
                turn_xn2(st)
                maxima_scores(st, 3)
                project_output(st, 0)
                scores(st, 3)
                values(st, 3)
                turn_output(st, 0)
                gate_and_up(st, 0)
                maxima_scores(st, 4)
                project_v(st)
                scores(st, 4)
                values(st, 4)
                gate_and_up(st, 1)
                maxima_scores(st, 5)
                scores(st, 5)
                turn_values(st, 1)
                values(st, 5)
                turn_maxima(st, 1)
                maxima_scores(st, 6)
                gate_and_up(st, 2)
                scores(st, 6)
                project_output(st, 1)
                values(st, 6)
                turn_inputs(st)
                maxima_scores(st, 7)
                scores(st, 7)
                values(st, 7)
                turn_output(st, 1)

            pe.wait_ge(ident_set, 2)
            pe.wait_ge(w_qk_in, 2 * DMA)
            for w in range(2):
                pe.transpose(ps_q[:, D * w:D * (w + 1)], w_nat[:, w, :], ident[:, :])
            pe.wait_ge(consts_set, 4)
            pe.wait_ge(rows_set, 2)
            for w in range(2):
                pe.matmul(ps_m[:, w:w + 1], b_row_p[0:1, w, :], one[0:1, 0:1], start=True, stop=True)
                for g in range(GRP):
                    at = 2 + GRP * w + g
                    mm = pe.matmul(ps_m[0:ROWS, at:at + 1], b_row_p[0:1, w, ROWS * g:ROWS * (g + 1)],
                                   one[0:1, 0:1], start=True, stop=True)
            mm.then_inc(qk_w_turned, 1)
            step(Step(-2, 1, NB))
            pe.wait_ge(w_vo_in, 2 * DMA)
            for w in range(2):
                mm = pe.transpose(ps_t[:, D * w:D * (w + 1)], w_nat[:, 2 + w, :], ident[:, :])
            mm.then_inc(vo_w_turned, 1)
            pe.wait_ge(qk_w_ready, 4)
            step(Step(-1, 0, NB))
            pe.wait_ge(vo_w_ready, 2)
            pe.wait_ge(bv_set, 1)
            pe.matmul(ps_a[:, 0:D], bv_wide[:, :], woT[:, :], start=True, stop=True).then_inc(bias_summed, 1)
            pe.wait_ge(bias_ready, 1)
            step(Step(-1, 1, NB))
            pe.wait_ge(ffn_w_f32, 2)
            for t in range(HID_T):
                for w in range(2):
                    pe.transpose((ps_b, ps_m)[w][:, D * t:D * (t + 1)], gu_nat[:, w, t, :], ident[:, :])
                mm = pe.transpose(ps_o[:, D * t:D * (t + 1)], dn_nat[:, t, :], ident[:, :])
            mm.then_inc(ffn_w_turned, 1)
            pe.wait_ge(dn_w_ready, 1)
            pe.wait_ge(gu_w_ready, 2)
            pe.wait_ge(ones_set, 1)
            run(pe, step, 0, LAST, LOOP_FIRST, LOOP_LAST)


INPUTS = ["x", "ctx_1024", "g_xattn", "g_ffn", "L0_xattn_Wq", "L0_xattn_bq", "L0_xattn_Wk", "L0_xattn_bk",
          "L0_xattn_Wv", "L0_xattn_bv", "L0_xattn_Wo", "L0_xattn_bo", "L0_ffn_w_gate", "L0_ffn_w_up",
          "L0_ffn_w_down"]


def kernel(**inputs):
    import numpy as np
    import concourse.bacc as bacc
    from concourse.bass_utils import run_bass_kernel_spmd

    nc = bacc.Bacc("TRN2", target_bir_lowering=False, num_devices=1)
    arrays, args = {}, []
    for name in INPUTS:
        a = np.ascontiguousarray(inputs[name])
        arrays[f"in_{name}"] = a
        args.append(nc.dram_tensor(f"in_{name}", a.shape, mybir.dt.from_np(a.dtype), kind="ExternalInput").ap())
    shape = arrays["in_x"].shape
    out = nc.dram_tensor("out_x", shape, F32, kind="ExternalOutput").ap()
    build(nc, *args, out)
    result = run_bass_kernel_spmd(nc, [arrays], core_ids=[0])
    return result.results[0]["out_x"]
```
